# Optimizing a Trainium2 kernel written in Bass

```python
import numpy as np
import jax
import jax.numpy as jnp

def _softmax(x, axis=-1):
    return jax.nn.softmax(x, axis=axis)

def _gelu(x):
    return jax.nn.gelu(x, approximate=True)

def _silu(x):
    return jax.nn.silu(x)

def _sigmoid(x):
    return jax.nn.sigmoid(x)

def _layernorm(x, axis=-1, eps=1e-05):
    m = jnp.mean(x, axis=axis, keepdims=True)
    v = jnp.var(x, axis=axis, keepdims=True)
    return (x - m) / jnp.sqrt(v + eps)

def _scatter_add(tgt, idx, src, axis=0):
    return tgt.at[idx].add(src)

def _segment_sum(src, seg, n):
    return jax.ops.segment_sum(src, seg, n)
kernel_name = 'mk_dlrm_tower_d1_rec_r8_552134'

def setup_inputs(seed: int=0):
    np.random.seed(seed)
    _w = jnp.asarray

    def _rec_inputs():
        import jax
        import jax.numpy as jnp
        _tk = jax.random.key(seed)
        ids = jnp.stack([jax.random.randint(jax.random.fold_in(_tk, 200 + f), (2048,), 0, v, jnp.int32) for f, v in enumerate([12500, 125000, 1000, 12500, 1000, 12500, 1000, 1000, 1000, 1250, 1000, 1250, 12500, 1250, 1000, 12500, 1000, 1250, 1000, 12500, 12500, 1000, 12500, 12500, 1000, 1000])], axis=1)
        tbl_0 = 0.05 * jax.random.normal(jax.random.fold_in(_tk, 500 + 0), (12500, 128), jnp.float32)
        tbl_1 = 0.05 * jax.random.normal(jax.random.fold_in(_tk, 500 + 1), (125000, 128), jnp.float32)
        tbl_2 = 0.05 * jax.random.normal(jax.random.fold_in(_tk, 500 + 2), (1000, 128), jnp.float32)
        tbl_3 = 0.05 * jax.random.normal(jax.random.fold_in(_tk, 500 + 3), (12500, 128), jnp.float32)
        tbl_4 = 0.05 * jax.random.normal(jax.random.fold_in(_tk, 500 + 4), (1000, 128), jnp.float32)
        tbl_5 = 0.05 * jax.random.normal(jax.random.fold_in(_tk, 500 + 5), (12500, 128), jnp.float32)
        tbl_6 = 0.05 * jax.random.normal(jax.random.fold_in(_tk, 500 + 6), (1000, 128), jnp.float32)
        tbl_7 = 0.05 * jax.random.normal(jax.random.fold_in(_tk, 500 + 7), (1000, 128), jnp.float32)
        tbl_8 = 0.05 * jax.random.normal(jax.random.fold_in(_tk, 500 + 8), (1000, 128), jnp.float32)
        tbl_9 = 0.05 * jax.random.normal(jax.random.fold_in(_tk, 500 + 9), (1250, 128), jnp.float32)
        tbl_10 = 0.05 * jax.random.normal(jax.random.fold_in(_tk, 500 + 10), (1000, 128), jnp.float32)
        tbl_11 = 0.05 * jax.random.normal(jax.random.fold_in(_tk, 500 + 11), (1250, 128), jnp.float32)
        tbl_12 = 0.05 * jax.random.normal(jax.random.fold_in(_tk, 500 + 12), (12500, 128), jnp.float32)
        tbl_13 = 0.05 * jax.random.normal(jax.random.fold_in(_tk, 500 + 13), (1250, 128), jnp.float32)
        tbl_14 = 0.05 * jax.random.normal(jax.random.fold_in(_tk, 500 + 14), (1000, 128), jnp.float32)
        tbl_15 = 0.05 * jax.random.normal(jax.random.fold_in(_tk, 500 + 15), (12500, 128), jnp.float32)
        tbl_16 = 0.05 * jax.random.normal(jax.random.fold_in(_tk, 500 + 16), (1000, 128), jnp.float32)
        tbl_17 = 0.05 * jax.random.normal(jax.random.fold_in(_tk, 500 + 17), (1250, 128), jnp.float32)
        tbl_18 = 0.05 * jax.random.normal(jax.random.fold_in(_tk, 500 + 18), (1000, 128), jnp.float32)
        tbl_19 = 0.05 * jax.random.normal(jax.random.fold_in(_tk, 500 + 19), (12500, 128), jnp.float32)
        tbl_20 = 0.05 * jax.random.normal(jax.random.fold_in(_tk, 500 + 20), (12500, 128), jnp.float32)
        tbl_21 = 0.05 * jax.random.normal(jax.random.fold_in(_tk, 500 + 21), (1000, 128), jnp.float32)
        tbl_22 = 0.05 * jax.random.normal(jax.random.fold_in(_tk, 500 + 22), (12500, 128), jnp.float32)
        tbl_23 = 0.05 * jax.random.normal(jax.random.fold_in(_tk, 500 + 23), (12500, 128), jnp.float32)
        tbl_24 = 0.05 * jax.random.normal(jax.random.fold_in(_tk, 500 + 24), (1000, 128), jnp.float32)
        tbl_25 = 0.05 * jax.random.normal(jax.random.fold_in(_tk, 500 + 25), (1000, 128), jnp.float32)
        _rk = jax.random.fold_in(_tk, 7)
        r_dense_features = -0.000520686 + 1.00062 * jax.random.normal(jax.random.fold_in(_rk, 101), (2048, 128), jnp.float32)
        W_top1 = 0.0405887 * jax.random.normal(jax.random.fold_in(_tk, 801), (607, 512), jnp.float32)
        W_top2 = 0.0441942 * jax.random.normal(jax.random.fold_in(_tk, 802), (512, 256), jnp.float32)
        W_top3 = 0.0625 * jax.random.normal(jax.random.fold_in(_tk, 803), (256, 1), jnp.float32)
        b_top1 = jnp.zeros((512,), jnp.float32)
        b_top2 = jnp.zeros((256,), jnp.float32)
        return (r_dense_features, ids, tbl_0, tbl_1, tbl_2, tbl_3, tbl_4, tbl_5, tbl_6, tbl_7, tbl_8, tbl_9, tbl_10, tbl_11, tbl_12, tbl_13, tbl_14, tbl_15, tbl_16, tbl_17, tbl_18, tbl_19, tbl_20, tbl_21, tbl_22, tbl_23, tbl_24, tbl_25, W_top1, b_top1, W_top2, b_top2, W_top3)
    r_dense_features, ids, tbl_0, tbl_1, tbl_2, tbl_3, tbl_4, tbl_5, tbl_6, tbl_7, tbl_8, tbl_9, tbl_10, tbl_11, tbl_12, tbl_13, tbl_14, tbl_15, tbl_16, tbl_17, tbl_18, tbl_19, tbl_20, tbl_21, tbl_22, tbl_23, tbl_24, tbl_25, W_top1, b_top1, W_top2, b_top2, W_top3 = _rec_inputs()

    def _L0_rec_setup():
        import jax, jax.numpy as jnp
        import numpy as np
        B, F, D = (2048, 26, 128)
        key = jax.random.key(seed)
        k1, k2 = jax.random.split(key)
        dense_features = jax.random.normal(k1, (B, D), dtype=jnp.float32)
        sparse_values = jax.random.normal(k2, (B, F, D), dtype=jnp.float32)
        return {'dense_features': dense_features, 'sparse_values': sparse_values}
    _L0_rec_all = _L0_rec_setup()
    _L0_rec_in = {k: v for k, v in _L0_rec_all.items() if k in ()}
    del _L0_rec_all
    return {'r_dense_features': r_dense_features, 'ids': ids, 'tbl_0': tbl_0, 'tbl_1': tbl_1, 'tbl_2': tbl_2, 'tbl_3': tbl_3, 'tbl_4': tbl_4, 'tbl_5': tbl_5, 'tbl_6': tbl_6, 'tbl_7': tbl_7, 'tbl_8': tbl_8, 'tbl_9': tbl_9, 'tbl_10': tbl_10, 'tbl_11': tbl_11, 'tbl_12': tbl_12, 'tbl_13': tbl_13, 'tbl_14': tbl_14, 'tbl_15': tbl_15, 'tbl_16': tbl_16, 'tbl_17': tbl_17, 'tbl_18': tbl_18, 'tbl_19': tbl_19, 'tbl_20': tbl_20, 'tbl_21': tbl_21, 'tbl_22': tbl_22, 'tbl_23': tbl_23, 'tbl_24': tbl_24, 'tbl_25': tbl_25, 'W_top1': W_top1, 'b_top1': b_top1, 'W_top2': W_top2, 'b_top2': b_top2, 'W_top3': W_top3}

def reference(r_dense_features, ids, tbl_0, tbl_1, tbl_2, tbl_3, tbl_4, tbl_5, tbl_6, tbl_7, tbl_8, tbl_9, tbl_10, tbl_11, tbl_12, tbl_13, tbl_14, tbl_15, tbl_16, tbl_17, tbl_18, tbl_19, tbl_20, tbl_21, tbl_22, tbl_23, tbl_24, tbl_25, W_top1, b_top1, W_top2, b_top2, W_top3):
    import jax
    import jax.numpy as jnp

    def _L0_rec_ref(dense_features, sparse_values):
        import jax, jax.numpy as jnp
        import numpy as np
        B, F, D = (2048, 26, 128)
        sd = jnp.einsum('bfd,bd->bf', sparse_values, dense_features)
        ss = jnp.einsum('bfd,bgd->bfg', sparse_values, sparse_values)
        iu, ju = jnp.triu_indices(F, k=1)
        pairs = ss[:, iu, ju]
        return jnp.concatenate([dense_features, sd, pairs], axis=1)
    e = jnp.stack([tbl_0[ids[:, 0]], tbl_1[ids[:, 1]], tbl_2[ids[:, 2]], tbl_3[ids[:, 3]], tbl_4[ids[:, 4]], tbl_5[ids[:, 5]], tbl_6[ids[:, 6]], tbl_7[ids[:, 7]], tbl_8[ids[:, 8]], tbl_9[ids[:, 9]], tbl_10[ids[:, 10]], tbl_11[ids[:, 11]], tbl_12[ids[:, 12]], tbl_13[ids[:, 13]], tbl_14[ids[:, 14]], tbl_15[ids[:, 15]], tbl_16[ids[:, 16]], tbl_17[ids[:, 17]], tbl_18[ids[:, 18]], tbl_19[ids[:, 19]], tbl_20[ids[:, 20]], tbl_21[ids[:, 21]], tbl_22[ids[:, 22]], tbl_23[ids[:, 23]], tbl_24[ids[:, 24]], tbl_25[ids[:, 25]]], axis=1)
    z = _L0_rec_ref(r_dense_features, e)
    z = z.reshape(z.shape[0], -1)
    h = jnp.concatenate([z, r_dense_features], axis=1)
    h = jnp.maximum(h @ W_top1 + b_top1, 0.0)
    h = jnp.maximum(h @ W_top2 + b_top2, 0.0)
    y = h @ W_top3
    return y

_drawn_inputs = setup_inputs


def setup_inputs(seed=0):
    import zlib

    import numpy as np

    out = dict(_drawn_inputs(seed))
    spreads = {'b_top1': (0.0, 0.1), 'b_top2': (0.0, 0.1)}
    factors = {}
    for name, (base, spread) in spreads.items():
        noise = np.random.default_rng([zlib.crc32(name.encode()), seed]).standard_normal(out[name].shape)
        drawn = base * np.exp(spread * noise) if base else spread * noise
        out[name] = jnp.asarray(drawn.astype(out[name].dtype))
    for name, factor in factors.items():
        out[name] = (out[name] * factor).astype(out[name].dtype)
    return out
```

```python
from contextlib import ExitStack

import numpy as np

import concourse.bass as bass
from concourse import mybir

ALU = mybir.AluOpType
ACT = mybir.ActivationFunctionType
F32 = mybir.dt.float32
F32R = mybir.dt.float32r
I32 = mybir.dt.int32

P = 128
FEATURES = 26
VECTORS = FEATURES + 1
SLOT = 32
QUAD = P // SLOT
GROUPS = 4
JJ = -(-VECTORS // GROUPS)
SUBS = 2
TILE = SUBS * P
BATCHES = 4
BQ = P // QUAD // BATCHES
UPPER1, UPPER2 = 512, 256
M1, M2 = UPPER1 // P, UPPER2 // P

LOOKED_UP = [2, 4, 6, 7, 8]
GATHERED = [f for f in range(FEATURES) if f not in LOOKED_UP]
ORDER = LOOKED_UP + GATHERED + [FEATURES]
NL, NG = len(LOOKED_UP), len(GATHERED)
CHUNKS = 8
HALVES = 2
HC = CHUNKS // HALVES
RING = 2

LB = -(-NL // 2)
GB = -(-(NG + 1) // 4)
BLOCKS = LB + SUBS * GB

TURNED_AFTER_STEP = [[0, 1], [2, 3], [4, 5]]
TURNED_AFTER_BATCH = [[], [], [], [0, 1, 2, 3, 4, 5]]

ACT_SAMPLES, DVE_SAMPLES = (0, 1, 2), (3,)

FREE = 1
BANKS = 2


def gathered_block(u, g):
    return LB + u * GB + g


def looked_up_block(l):
    return l // 2


def ends_block(l):
    return l % 2 == 1 or l == NL - 1


LAST_OF_ROWS = [gathered_block(u, GB - 1) for u in range(SUBS)]


def bank_of(block):
    return block % 2


def blocks_in(bank, blocks=BLOCKS):
    return (blocks - bank + 1) // 2


def bank_uses(t, block):
    return t * blocks_in(bank_of(block)) + blocks_in(bank_of(block), block)


def gathered_vectors(g):
    return range(4 * g, min(4 * g + 4, NG + 1))


STEPS = M1 + M2 + 1


def build_dlrm_tower(nc, ids, looked_ids, dense, tables, small_tables, w1_pairs, w1_dense, b1, w2, b2, w3, eye,
                     row_numbers, out):
    tiles = dense.shape[0] // TILE
    ctx = ExitStack()
    with ctx:
        def sb(name, shape, dt):
            return ctx.enter_context(nc.sbuf_tensor(name, shape, dt))

        def psum(name, shape):
            return ctx.enter_context(nc.psum_tensor(name, shape, F32))

        def sem(name):
            return ctx.enter_context(nc.semaphore(name))

        w1_hi = sb("w1_hi", [P, JJ, UPPER1], F32R)
        w1_lo = sb("w1_lo", [P, JJ, UPPER1], F32R)
        wd_raw = sb("wd_raw", [P, 2, UPPER1], F32)
        w2_raw = sb("w2_raw", [P, M1, UPPER2], F32)
        wd_sum = sb("wd_sum", [P, UPPER1], F32)
        wd_hi = sb("wd_hi", [P, UPPER1], F32R)
        wd_lo = sb("wd_lo", [P, UPPER1], F32R)
        w2_hi = sb("w2_hi", [P, M1, UPPER2], F32R)
        w2_lo = sb("w2_lo", [P, M1, UPPER2], F32R)
        w3_sb = sb("w3_sb", [P, M2], F32)
        b1_sb = sb("b1_sb", [P, M1], F32)
        b2_sb = sb("b2_sb", [P, M2], F32)
        eye_sb = sb("eye_sb", [P, P], F32)
        rown_sb = sb("rown_sb", [P, CHUNKS], F32)
        table_hi = sb("table_hi", [P, NL, CHUNKS, P], F32R)
        table_lo = sb("table_lo", [P, NL, CHUNKS, P], F32R)

        idx = [sb(f"idx{u}", [P, FEATURES], I32) for u in range(SUBS)]
        spread = sb("spread", [P, NL, TILE], I32)
        onehot = sb("onehot", [P, RING, CHUNKS, TILE], F32R)
        rows = [sb(f"rows{u}", [P, NG + 1, P], F32) for u in range(SUBS)]
        vectors = sb("vectors", [P, TILE, SLOT], F32)
        x_hi = sb("x_hi", [P, TILE], F32R)
        x_lo = sb("x_lo", [P, TILE], F32R)
        pairs_hi = sb("pairs_hi", [P, JJ, TILE], F32R)
        pairs_lo = sb("pairs_lo", [P, JJ, TILE], F32R)
        r1_hi = sb("r1_hi", [P, M1, TILE], F32R)
        r1_lo = sb("r1_lo", [P, M1, TILE], F32R)

        work = sb("work", [P, SUBS * JJ * P + (M1 + M2 + 1) * TILE], F32)
        at = SUBS * JJ * P
        pairs = [work[:, u * JJ * P:(u + 1) * JJ * P].rearrange("p (k s) -> p k s", k=JJ)
                 for u in range(SUBS)]
        r1 = work[:, at:at + M1 * TILE].rearrange("p (m s) -> p m s", m=M1)
        r2 = work[:, at + M1 * TILE:at + (M1 + M2) * TILE].rearrange("p (m s) -> p m s", m=M2)
        y = work[0:1, at + (M1 + M2) * TILE:at + (M1 + M2 + 1) * TILE]
        w1_raw = work[:, 0:JJ * UPPER1].rearrange("p (k n) -> p k n", k=JJ)

        stage = vectors[:].rearrange("p s v -> p (s v)")
        one = CHUNKS * P
        in_vectors = [stage[:, i * one:(i + 1) * one] for i in range(2)]
        in_rows = [rows[1][:].rearrange("p v d -> p (v d)")[:, i * one:(i + 1) * one] for i in range(2)]
        in_work = [work[:, i * one:(i + 1) * one] for i in range(NL - 4)]
        table_raw = [x.rearrange("p (c d) -> p c d", c=CHUNKS) for x in in_vectors + in_rows + in_work]

        ps_v = [psum(f"ps_v{b}", [P, 512]) for b in range(2)]
        ps_g = [psum(f"ps_g{b}", [P, BQ, P]) for b in range(2)]
        ps_h = [psum(f"ps_h{b}", [P, 512]) for b in range(2)]

        rown_in = sem("rown_in")
        eye_in = sem("eye_in")
        table_in = [sem(f"table_in{l}") for l in range(NL)]
        small_weights_in = sem("small_weights_in")
        w1_in = sem("w1_in")
        rounded = sem("rounded")
        summed = sem("summed")
        table_split = sem("table_split")
        work_free = sem("work_free")
        weights_split = sem("weights_split")
        w1_split = sem("w1_split")
        pads_zeroed = sem("pads_zeroed")
        idx_in = [sem(f"idx_in{u}") for u in range(SUBS)]
        dense_in = [sem(f"dense_in{u}") for u in range(SUBS)]
        rows_in = [sem(f"rows_in{u}") for u in range(SUBS)]
        rows_used = [sem(f"rows_used{u}") for u in range(SUBS)]
        gathering = sem("gathering")
        spread_in = sem("spread_in")
        onehot_made = sem("onehot_made")
        onehot_used = sem("onehot_used")
        turned = [sem(f"turned{b}") for b in range(2)]
        vectors_out = [sem(f"vectors_out{b}") for b in range(2)]
        x_hi_out = sem("x_hi_out")
        products = [sem(f"products{b}") for b in range(2)]
        act_moved = sem("act_moved")
        dve_moved = sem("dve_moved")
        pairs_hi_out = sem("pairs_hi_out")
        pairs_split = sem("pairs_split")
        layer = [sem(f"layer{b}") for b in range(2)]
        layer_read = [sem(f"layer_read{b}") for b in range(2)]
        r1_split = sem("r1_split")
        stored = sem("stored")
        y_sent = sem("y_sent")

        block = ctx.enter_context(nc.Block())

        @block.sync
        def _(sp):
            def samples(x, n, ahead, u=0, count=TILE):
                return x[ahead * TILE + u * P:, :][bass.ds(n * TILE, count), :]

            def load_spread(n, ahead):
                sp.dma_start(spread[:], looked_ids[:, ahead * TILE:][:, bass.ds(n * TILE, TILE)]
                             .partition_broadcast(P)).then_inc(spread_in, 16)

            def load_idx(n, ahead, u):
                sp.dma_start(idx[u][:], samples(ids, n, ahead, u, P)).then_inc(idx_in[u], 16)

            def load_dense(n, ahead, u):
                sp.dma_start(rows[u][:, NG, :], samples(dense, n, ahead, u, P)).then_inc(dense_in[u], 16)

            def store(n, ahead):
                bank = (STEPS - 1) % 2
                sp.wait_ge(layer_read[bank], n * blocks_in(bank, STEPS)
                           + ((ahead + 1) * blocks_in(bank, STEPS) + FREE))
                sp.dma_start(samples(out, n, ahead).rearrange("b o -> o b"), y).then_inc(stored, 16)
                sp.wait_ge(stored, n * 16 + (ahead + 1) * 16)
                sp.sem_inc(y_sent, 1)

            sp.sem_inc(y_sent, FREE)
            load_idx(0, 0, 0)
            load_spread(0, 0)
            sp.dma_start(rown_sb[:], row_numbers).then_inc(rown_in, 16)
            for l in range(NL):
                sp.dma_start(table_raw[l], small_tables[:, l]).then_inc(table_in[l], 16)
                if l == 1:
                    load_idx(0, 0, 1)
                    sp.dma_start(eye_sb[:], eye).then_inc(eye_in, 16)
                if l == 3:
                    sp.dma_start(wd_raw[:], w1_dense).then_inc(small_weights_in, 16)
                    sp.dma_start(w2_raw[:], w2.rearrange("(k p) n -> p k n", p=P)).then_inc(small_weights_in, 16)
            load_dense(0, 0, 0)
            sp.wait_ge(rows_used[1], FREE)
            load_dense(0, 0, 1)
            sp.wait_ge(work_free, 1)
            sp.dma_start(w1_raw, w1_pairs).then_inc(w1_in, 16)
            def load_next(n, ahead, u):
                sp.wait_ge(rows_in[u], n * (16 * NG) + ahead * (16 * NG))
                load_idx(n, ahead, u)
                sp.wait_ge(rows_used[u], n + (ahead + FREE))
                load_dense(n, ahead, u)

            def load_next_spread(n, ahead):
                sp.wait_ge(onehot_made, n * (NL * HALVES) + ahead * (NL * HALVES))
                load_spread(n, ahead)

            load_next(0, 1, 0)
            load_next_spread(0, 1)
            load_next(0, 1, 1)
            load_next(0, 2, 0)
            load_next_spread(0, 2)
            store(0, 0)
            load_next(0, 2, 1)
            with sp.Fori(0, tiles - 3) as t:
                load_next(t, 3, 0)
                load_next_spread(t, 3)
                store(t, 1)
                load_next(t, 3, 1)
            store(0, tiles - 2)
            store(0, tiles - 1)

        @block.gpsimd
        def _(pool):
            with pool.Fori(0, tiles) as t:
                for u in range(SUBS):
                    pool.wait_ge(idx_in[u], t * 16 + 16)
                    pool.wait_ge(rows_used[u], t + FREE)
                    pool.sem_inc(gathering, 1)
                    for n, f in enumerate(GATHERED):
                        nc.gpsimd.indirect_dma_start(
                            rows[u][:, n, :], None, tables[f],
                            bass.IndirectOffsetOnAxis(ap=idx[u][:, f:f + 1], axis=0),
                        ).then_inc(rows_in[u], 16)

        @block.tensor
        def _(pe):
            def bank_free(t, b):
                pe.wait_ge(vectors_out[bank_of(b)], bank_uses(t, b) + FREE)

            def look_up(t, l):
                b = looked_up_block(l)
                if l % 2 == 0:
                    bank_free(t, b)
                to = ps_v[bank_of(b)][:, (l % 2) * TILE:(l % 2 + 1) * TILE]
                for c in range(CHUNKS):
                    if c % HC == 0:
                        pe.wait_ge(onehot_made, t * (NL * HALVES) + (l * HALVES + c // HC + 1))
                    nc.tensor.matmul(to, table_hi[:, l, c, :], onehot[:, l % RING, c, :], start=c == 0, stop=False)
                    last = nc.tensor.matmul(to, table_lo[:, l, c, :], onehot[:, l % RING, c, :],
                                            start=False, stop=c == CHUNKS - 1)
                    if c % HC == HC - 1:
                        last.then_inc(turned[bank_of(b)] if ends_block(l) and c == CHUNKS - 1 else onehot_used, 1)

            def turn(t, u, some):
                for g in some:
                    if g == 0:
                        pe.wait_ge(rows_in[u], t * (16 * NG) + 16 * NG)
                        pe.wait_ge(dense_in[u], t * 16 + 16)
                    b = gathered_block(u, g)
                    bank_free(t, b)
                    for n, v in enumerate(gathered_vectors(g)):
                        last = nc.tensor.transpose(ps_v[bank_of(b)][:, n * P:(n + 1) * P],
                                                   rows[u][:, v, :], eye_sb[:])
                    last.then_inc(turned[bank_of(b)], 1)

            def vectors_ready(t, u):
                ready = gathered_block(u + 1, 0)
                for bank in range(2):
                    pe.wait_ge(vectors_out[bank], t * blocks_in(bank) + (blocks_in(bank, ready) + FREE))

            def multiply_pairs(t, u, k):
                before = t * (SUBS * BATCHES) + (u * BATCHES + k - 1 + BANKS)
                pe.wait_ge(act_moved, before)
                pe.wait_ge(dve_moved, before)
                for q in range(BQ):
                    s = u * P + (k * BQ + q) * QUAD
                    last = nc.tensor.matmul(
                        ps_g[k % 2][:, q, 0:QUAD * VECTORS],
                        vectors[:, s:s + QUAD, :].rearrange("p s v -> p (s v)"),
                        vectors[:, s:s + QUAD, 0:VECTORS], start=True, stop=True)
                last.then_inc(products[k % 2], 1)

            def tower_step(t, step, terms, m=P):
                bank = step % 2
                pe.wait_ge(layer_read[bank], t * blocks_in(bank, STEPS) + (step // 2 + FREE))
                for n, (stationary, moving) in enumerate(terms):
                    last = nc.tensor.matmul(ps_h[bank][0:m, 0:TILE], stationary, moving,
                                            start=n == 0, stop=n == len(terms) - 1)
                last.then_inc(layer[bank], 1)

            def three(w_hi, w_lo, a_hi, a_lo):
                return [(w_hi, a_hi), (w_lo, a_hi), (w_hi, a_lo)]

            def layer1(t, m):
                if m == 0:
                    pe.wait_ge(pairs_split, t * (SUBS * 2) + SUBS * 2)
                c = slice(m * P, m * P + P)
                terms = three(wd_hi[:, c], wd_lo[:, c], x_hi[:], x_lo[:])
                for k in range(JJ):
                    terms += three(w1_hi[:, k, c], w1_lo[:, k, c], pairs_hi[:, k, :], pairs_lo[:, k, :])
                tower_step(t, m, terms)

            def layer2(t, m):
                if m == 0:
                    pe.wait_ge(r1_split, t * M1 + M1)
                c = slice(m * P, m * P + P)
                terms = []
                for k in range(M1):
                    terms += three(w2_hi[:, k, c], w2_lo[:, k, c], r1_hi[:, k, :], r1_lo[:, k, :])
                tower_step(t, M1 + m, terms)

            def layer3(t):
                for step in range(M1, M1 + M2):
                    pe.wait_ge(layer_read[step % 2], t * blocks_in(step % 2, STEPS) + (step // 2 + 1 + FREE))
                tower_step(t, M1 + M2, [(w3_sb[:, m:m + 1], r2[:, m, :]) for m in range(M2)], m=1)

            for l in range(NL):
                pe.wait_ge(table_split, l + 1)
                look_up(0, l)
            pe.wait_ge(eye_in, 16)
            turn(0, 0, range(GB))
            pe.wait_ge(pads_zeroed, 1)
            vectors_ready(0, 0)
            for k in range(BATCHES):
                multiply_pairs(0, 0, k)
            turn(0, 1, range(GB))
            pe.wait_ge(weights_split, 1)
            with pe.Fori(0, tiles - 1) as t:
                vectors_ready(t, 1)
                for k in range(BATCHES):
                    multiply_pairs(t, 1, k)
                look_up(t + 1, 0)
                look_up(t + 1, 1)
                layer1(t, 0)
                look_up(t + 1, 2)
                layer1(t, 1)
                look_up(t + 1, 3)
                layer1(t, 2)
                layer1(t, 3)
                look_up(t + 1, 4)
                layer2(t, 0)
                turn(t + 1, 0, TURNED_AFTER_STEP[0])
                layer2(t, 1)
                turn(t + 1, 0, TURNED_AFTER_STEP[1])
                layer3(t)
                turn(t + 1, 0, TURNED_AFTER_STEP[2])
                vectors_ready(t + 1, 0)
                for k in range(BATCHES):
                    multiply_pairs(t + 1, 0, k)
                    turn(t + 1, 1, TURNED_AFTER_BATCH[k])
            vectors_ready(tiles - 1, 1)
            for k in range(BATCHES):
                multiply_pairs(tiles - 1, 1, k)
            for m in range(M1):
                layer1(tiles - 1, m)
            for m in range(M2):
                layer2(tiles - 1, m)
            layer3(tiles - 1)

        def block_places(b):
            bank = ps_v[bank_of(b)]
            if b < LB:
                n = min(2, NL - 2 * b)
                return (bank[:, 0:n * TILE].rearrange("p (v s) -> p v s", v=n),
                        vectors[:, :, 2 * b:2 * b + n].rearrange("p s v -> p v s"))
            u, g = divmod(b - LB, GB)
            n, first = len(gathered_vectors(g)), NL + 4 * g
            return (bank[:, 0:n * P].rearrange("p (v s) -> p v s", v=n),
                    vectors[:, u * P:(u + 1) * P, first:first + n].rearrange("p s v -> p v s"))

        def share(u, k, s, g):
            n = len(range(g, VECTORS, GROUPS))
            frm = ps_g[k % 2][SLOT * s:SLOT * s + SLOT, :, s * VECTORS + g:(s + 1) * VECTORS:GROUPS]
            first = k * BQ * QUAD + s
            to = pairs[u][SLOT * g:SLOT * g + SLOT, 0:n, first:first + (BQ - 1) * QUAD + 1:QUAD]
            return to, frm.rearrange("p q j -> p j q")

        @block.scalar
        def _(act):
            def block_out(t, b):
                if bank_of(b) == 0:
                    act.wait_ge(turned[0], bank_uses(t, b) + 1)
                    if b in LAST_OF_ROWS:
                        act.sem_inc(rows_used[LAST_OF_ROWS.index(b)], 1)
                    frm, to = block_places(b)
                    nc.scalar.copy(to, frm).then_inc(vectors_out[0], 1)

            def dense_out(t, u):
                b = gathered_block(u, GB - 1)
                act.wait_ge(vectors_out[bank_of(b)], bank_uses(t, b) + (1 + FREE))
                nc.scalar.copy(x_hi[:, u * P:(u + 1) * P], vectors[:, u * P:(u + 1) * P, VECTORS - 1]
                               ).then_inc(x_hi_out, 1)

            def move(t, u, k):
                act.wait_ge(products[k % 2], t * (SUBS * 2) + (u * 2 + k // 2 + 1))
                for s in ACT_SAMPLES:
                    for g in range(GROUPS):
                        last = nc.scalar.copy(*share(u, k, s, g))
                last.then_inc(act_moved, 1)

            def round_pairs(t, u, h):
                moved = u * BATCHES + (h + 1) * BATCHES // 2 + BANKS
                act.wait_ge(act_moved, t * (SUBS * BATCHES) + moved)
                act.wait_ge(dve_moved, t * (SUBS * BATCHES) + moved)
                a, b = h * P // 2, (h + 1) * P // 2
                nc.scalar.copy(pairs_hi[:, :, u * P + a:u * P + b], pairs[u][:, :, a:b]).then_inc(pairs_hi_out, 1)

            def layer_out(t, step):
                bank = step % 2
                act.wait_ge(layer[bank], t * blocks_in(bank, STEPS) + (step // 2 + 1))
                frm = ps_h[bank][:, 0:TILE]
                if step < M1:
                    bias = b1_sb[:, step:step + 1]
                    nc.scalar.activation(r1[:, step, :], frm, ACT.Relu, bias=bias)
                    last = nc.scalar.activation(r1_hi[:, step, :], frm, ACT.Relu, bias=bias)
                elif step < M1 + M2:
                    m = step - M1
                    last = nc.scalar.activation(r2[:, m, :], frm, ACT.Relu, bias=b2_sb[:, m:m + 1])
                else:
                    act.wait_ge(y_sent, t + FREE)
                    last = nc.scalar.copy(y, ps_h[bank][0:1, 0:TILE])
                last.then_inc(layer_read[bank], 1)

            act.sem_inc(rows_used[0], FREE)
            act.sem_inc(vectors_out[0], FREE)
            act.sem_inc(act_moved, BANKS)
            for bank in range(2):
                act.sem_inc(layer_read[bank], FREE)
            act.dma_start(w3_sb[:], w3).then_inc(small_weights_in, 16)
            act.dma_start(b1_sb[:], b1).then_inc(small_weights_in, 16)
            act.dma_start(b2_sb[:], b2).then_inc(small_weights_in, 16)
            for l in range(NL):
                act.wait_ge(table_in[l], 16)
                nc.scalar.copy(table_hi[:, l], table_raw[l]).then_inc(rounded, 1)
                if l == 1:
                    act.wait_ge(table_split, 2)
                if l == 3:
                    block_out(0, looked_up_block(0))
            act.wait_ge(small_weights_in, 16 * 5)
            nc.scalar.copy(w2_hi[:], w2_raw[:]).then_inc(rounded, 1)
            block_out(0, looked_up_block(4))
            act.wait_ge(w1_in, 16)
            nc.scalar.copy(w1_hi[:], w1_raw).then_inc(rounded, 1)
            for g in range(GB):
                block_out(0, gathered_block(0, g))
            dense_out(0, 0)
            act.wait_ge(summed, 1)
            nc.scalar.copy(wd_hi[:], wd_sum[:]).then_inc(rounded, 1)
            act.wait_ge(pads_zeroed, 2)
            for k in range(BATCHES):
                move(0, 0, k)
                if k % 2:
                    round_pairs(0, 0, k // 2)
            for g in range(GB):
                block_out(0, gathered_block(1, g))
            dense_out(0, 1)
            with act.Fori(0, tiles - 1) as t:
                for k in range(BATCHES):
                    move(t, 1, k)
                    if k % 2:
                        round_pairs(t, 1, k // 2)
                block_out(t + 1, looked_up_block(1))
                for m in range(M1):
                    layer_out(t, m)
                block_out(t + 1, looked_up_block(4))
                for n in range(3):
                    layer_out(t, M1 + n)
                    for g in TURNED_AFTER_STEP[n]:
                        block_out(t + 1, gathered_block(0, g))
                dense_out(t + 1, 0)
                for k in range(BATCHES):
                    move(t + 1, 0, k)
                    if k % 2:
                        round_pairs(t + 1, 0, k // 2)
                    for g in TURNED_AFTER_BATCH[k]:
                        block_out(t + 1, gathered_block(1, g))
                dense_out(t + 1, 1)
            for k in range(BATCHES):
                move(tiles - 1, 1, k)
                if k % 2:
                    round_pairs(tiles - 1, 1, k // 2)
            for step in range(STEPS):
                layer_out(tiles - 1, step)

        @block.vector
        def _(dve):
            def half_used(t, l, h):
                if ends_block(l) and h == HALVES - 1:
                    b = looked_up_block(l)
                    dve.wait_ge(turned[bank_of(b)], bank_uses(t, b) + 1)
                else:
                    dve.wait_ge(onehot_used, t * (NL * HALVES - LB) + (l * HALVES - l // 2 + h + 1))

            def make_onehot(t, l, halves=range(HALVES), first=False):
                for h in halves:
                    if l >= RING:
                        half_used(t, l - RING, h)
                    elif not first:
                        half_used(t - 1, max(i for i in range(NL) if i % RING == l), h)
                    for c in range(h * HC, (h + 1) * HC):
                        last = nc.vector.tensor_scalar(onehot[:, l % RING, c, :], spread[:, l, :], rown_sb[:, c:c + 1],
                                                       None, ALU.is_equal)
                    last.then_inc(onehot_made, 1)

            def block_out(t, b):
                if bank_of(b) == 1:
                    dve.wait_ge(turned[1], bank_uses(t, b) + 1)
                    if b in LAST_OF_ROWS:
                        dve.sem_inc(rows_used[LAST_OF_ROWS.index(b)], 1)
                    frm, to = block_places(b)
                    nc.vector.tensor_copy(to, frm).then_inc(vectors_out[1], 1)

            def dense_out(t, u):
                dve.wait_ge(x_hi_out, t * SUBS + (u + 1))
                nc.vector.tensor_tensor(x_lo[:, u * P:(u + 1) * P], vectors[:, u * P:(u + 1) * P, VECTORS - 1],
                                        x_hi[:, u * P:(u + 1) * P].bitcast(F32), ALU.subtract)

            def move(t, u, k):
                dve.wait_ge(products[k % 2], t * (SUBS * 2) + (u * 2 + k // 2 + 1))
                for s in DVE_SAMPLES:
                    for g in range(GROUPS):
                        last = nc.vector.tensor_copy(*share(u, k, s, g))
                last.then_inc(dve_moved, 1)

            def split_pairs(t, u, h):
                dve.wait_ge(pairs_hi_out, t * (SUBS * 2) + (u * 2 + h + 1))
                a, b = h * P // 2, (h + 1) * P // 2
                nc.vector.tensor_tensor(pairs_lo[:, :, u * P + a:u * P + b], pairs[u][:, :, a:b],
                                        pairs_hi[:, :, u * P + a:u * P + b].bitcast(F32), ALU.subtract
                                        ).then_inc(pairs_split, 1)

            def split_r1(t, m):
                dve.wait_ge(layer_read[m % 2], t * blocks_in(m % 2, STEPS) + (m // 2 + 1 + FREE))
                nc.vector.tensor_tensor(r1_lo[:, m, :], r1[:, m, :], r1_hi[:, m, :].bitcast(F32),
                                        ALU.subtract).then_inc(r1_split, 1)

            dve.sem_inc(vectors_out[1], FREE)
            dve.sem_inc(dve_moved, BANKS)
            def split_table(l, done):
                dve.wait_ge(rounded, done)
                nc.vector.tensor_tensor(table_lo[:, l], table_raw[l], table_hi[:, l].bitcast(F32),
                                        ALU.subtract).then_inc(table_split, 1)

            dve.wait_ge(rown_in, 16)
            dve.wait_ge(spread_in, 16)
            make_onehot(0, 0, first=True)
            split_table(0, 1)
            split_table(1, 2)
            make_onehot(0, 1, first=True)
            split_table(2, 3)
            make_onehot(0, 2)
            split_table(3, 4)
            dve.wait_ge(table_split, 4)
            dve.sem_inc(rows_used[1], FREE)
            make_onehot(0, 3)
            split_table(4, 5)
            dve.wait_ge(table_split, 5)
            dve.sem_inc(work_free, 1)
            make_onehot(0, 4)
            block_out(0, looked_up_block(3))
            for g in range(GB):
                block_out(0, gathered_block(0, g))
                if g == 1:
                    nc.vector.memset(vectors[:, :, VECTORS:SLOT], 0.0).then_inc(pads_zeroed, 1)
            dve.wait_ge(small_weights_in, 16 * 5)
            nc.vector.tensor_tensor(wd_sum[:], wd_raw[:, 0, :], wd_raw[:, 1, :], ALU.add).then_inc(summed, 1)
            dve.wait_ge(rounded, NL + 2)
            nc.vector.tensor_tensor(w1_lo[:], w1_raw, w1_hi[:].bitcast(F32), ALU.subtract).then_inc(w1_split, 1)
            dve.wait_ge(w1_split, 1)
            for u in range(SUBS):
                last = nc.vector.memset(pairs[u][SLOT * (GROUPS - 1):P, JJ - 1, :], 0.0)
            last.then_inc(pads_zeroed, 1)
            dense_out(0, 0)
            for k in range(BATCHES):
                move(0, 0, k)
                if k % 2:
                    split_pairs(0, 0, k // 2)
            nc.vector.tensor_tensor(w2_lo[:], w2_raw[:], w2_hi[:].bitcast(F32), ALU.subtract)
            dve.wait_ge(rounded, NL + 3)
            nc.vector.tensor_tensor(wd_lo[:], wd_sum[:], wd_hi[:].bitcast(F32), ALU.subtract).then_inc(weights_split, 1)
            for g in range(GB):
                block_out(0, gathered_block(1, g))
            dense_out(0, 1)
            with dve.Fori(0, tiles - 1) as t:
                dve.wait_ge(spread_in, t * 16 + 32)
                for k in range(BATCHES):
                    move(t, 1, k)
                    if k == 2:
                        split_pairs(t, 1, 0)
                    if k < 3:
                        make_onehot(t + 1, k // HALVES, [k % HALVES])
                split_pairs(t, 1, 1)
                make_onehot(t + 1, 1, [1])
                make_onehot(t + 1, 2)
                split_r1(t, 0)
                make_onehot(t + 1, 3)
                split_r1(t, 1)
                block_out(t + 1, looked_up_block(3))
                make_onehot(t + 1, 4)
                split_r1(t, 2)
                split_r1(t, 3)
                for g in sum(TURNED_AFTER_STEP, []):
                    block_out(t + 1, gathered_block(0, g))
                dense_out(t + 1, 0)
                for k in range(BATCHES):
                    move(t + 1, 0, k)
                    if k == 2:
                        split_pairs(t + 1, 0, 0)
                    for g in TURNED_AFTER_BATCH[k]:
                        block_out(t + 1, gathered_block(1, g))
                split_pairs(t + 1, 0, 1)
                dense_out(t + 1, 1)
            for k in range(BATCHES):
                move(tiles - 1, 1, k)
                if k % 2:
                    split_pairs(tiles - 1, 1, k // 2)
            for m in range(M1):
                split_r1(tiles - 1, m)



def pair_rows():
    row = {}
    at = P + FEATURES
    for i in range(FEATURES):
        row[i, FEATURES] = P + i
        for j in range(i + 1, FEATURES):
            row[i, j] = at
            at += 1
    where = np.full((JJ, GROUPS, SLOT), -1)
    for j in range(VECTORS):
        for i in range(j):
            where[j // GROUPS, j % GROUPS, i] = row[min(ORDER[i], ORDER[j]), max(ORDER[i], ORDER[j])]
    return where.reshape(JJ, P)


def kernel(**inputs):
    import concourse.bacc as bacc
    from concourse.bass_utils import run_bass_kernel_spmd

    a = {k: np.asarray(v) for k, v in inputs.items()}
    where = pair_rows()
    w1 = a["W_top1"]
    w1_pairs = np.zeros((JJ, P, UPPER1), w1.dtype)
    w1_pairs[where >= 0] = w1[where[where >= 0]]
    small = np.zeros((NL, CHUNKS * P, P), np.float32)
    for l, f in enumerate(LOOKED_UP):
        small[l, :len(a[f"tbl_{f}"])] = a[f"tbl_{f}"]
    data = {
        "ids": a["ids"],
        "looked_ids": np.ascontiguousarray(a["ids"][:, LOOKED_UP].T),
        "dense": a["r_dense_features"],
        "small_tables": np.ascontiguousarray(small.reshape(NL, CHUNKS, P, P).transpose(2, 0, 1, 3)),
        "w1_pairs": np.ascontiguousarray(w1_pairs.transpose(1, 0, 2)),
        "w1_dense": np.stack([w1[:P], w1[-P:]], axis=1),
        "b1": np.ascontiguousarray(a["b_top1"].reshape(M1, P).T),
        "w2": a["W_top2"],
        "b2": np.ascontiguousarray(a["b_top2"].reshape(M2, P).T),
        "w3": np.ascontiguousarray(a["W_top3"].reshape(M2, P).T),
        "eye": np.eye(P, dtype=np.float32),
        "row_numbers": np.arange(CHUNKS * P, dtype=np.float32).reshape(CHUNKS, P).T.copy(),
    }
    for f in GATHERED:
        data[f"tbl_{f}"] = a[f"tbl_{f}"]
    nc = bacc.Bacc("TRN2", target_bir_lowering=False, num_devices=1)
    d = {k: nc.dram_tensor(f"in_{k}", v.shape, mybir.dt.from_np(v.dtype), kind="ExternalInput").ap()
         for k, v in data.items()}
    out = nc.dram_tensor("out_y", (a["ids"].shape[0], 1), F32, kind="ExternalOutput").ap()
    build_dlrm_tower(nc, d["ids"], d["looked_ids"], d["dense"], {f: d[f"tbl_{f}"] for f in GATHERED}, d["small_tables"],
                     d["w1_pairs"], d["w1_dense"], d["b1"], d["w2"], d["b2"], d["w3"], d["eye"],
                     d["row_numbers"], out)
    r = run_bass_kernel_spmd(nc, [{f"in_{k}": v for k, v in data.items()}], core_ids=[0])
    return r.results[0]["out_y"]
```

```python
from contextlib import ExitStack

import numpy as np

import concourse.bass as bass
from concourse import mybir

ALU = mybir.AluOpType
ACT = mybir.ActivationFunctionType
F32 = mybir.dt.float32
F32R = mybir.dt.float32r
I32 = mybir.dt.int32

P = 128
FEATURES = 26
VECTORS = FEATURES + 1
SLOT = 32
QUAD = P // SLOT
TWICE = 3
SECOND = VECTORS
GROUPS = P // SLOT
JJ = (VECTORS - TWICE) // GROUPS
MOVING = VECTORS - 1
SUBS = 2
TILE = SUBS * P
BATCHES = 4
BQ = P // QUAD // BATCHES
UPPER1, UPPER2 = 512, 256
M1, M2 = UPPER1 // P, UPPER2 // P

LOOKED_UP = [2, 4, 6, 7, 8, 10]
GATHERED = [f for f in range(FEATURES) if f not in LOOKED_UP]
ORDER = LOOKED_UP + GATHERED + [FEATURES]
NL, NG = len(LOOKED_UP), len(GATHERED)
CHUNKS = 8
HALVES = 2
HC = CHUNKS // HALVES
RING = 2

LB = -(-NL // 2)
GB = -(-(NG + 1) // 4)
BLOCKS = LB + SUBS * GB

TURNED_AFTER_STEP = [[0, 1], [2, 3], [4, 5]]
TURNED_AFTER_BATCH = [[0, 1], [2, 3], [4, 5], []]

ACT_SAMPLES, DVE_SAMPLES = (0, 1, 2), (3,)

FREE = 1
BANKS = 2


def gathered_block(u, g):
    return LB + u * GB + g


def looked_up_block(l):
    return l // 2


def ends_block(l):
    return l % 2 == 1 or l == NL - 1


LAST_OF_ROWS = [gathered_block(u, GB - 1) for u in range(SUBS)]


def bank_of(block):
    return block % 2


def blocks_in(bank, blocks=BLOCKS):
    return (blocks - bank + 1) // 2


def bank_uses(t, block):
    return t * blocks_in(bank_of(block)) + blocks_in(bank_of(block), block)


def gathered_vectors(g):
    return range(4 * g, min(4 * g + 4, NG + 1))


def gathers(g):
    return min(4 * g + 4, NG) - 4 * g


STEPS = M1 + M2 + 1


def build_dlrm_tower(nc, ids, looked_ids, dense, tables, small_tables, w1_pairs, w1_dense, b1, w2, b2, w3, eye,
                     row_numbers, out):
    tiles = dense.shape[0] // TILE
    ctx = ExitStack()
    with ctx:
        def sb(name, shape, dt):
            return ctx.enter_context(nc.sbuf_tensor(name, shape, dt))

        def psum(name, shape):
            return ctx.enter_context(nc.psum_tensor(name, shape, F32))

        def sem(name):
            return ctx.enter_context(nc.semaphore(name))

        w1_hi = sb("w1_hi", [P, JJ, UPPER1], F32R)
        w1_lo = sb("w1_lo", [P, JJ, UPPER1], F32R)
        wd_raw = sb("wd_raw", [P, 2, UPPER1], F32)
        w2_raw = sb("w2_raw", [P, M1, UPPER2], F32)
        wd_sum = sb("wd_sum", [P, UPPER1], F32)
        wd_hi = sb("wd_hi", [P, UPPER1], F32R)
        wd_lo = sb("wd_lo", [P, UPPER1], F32R)
        w2_hi = sb("w2_hi", [P, M1, UPPER2], F32R)
        w2_lo = sb("w2_lo", [P, M1, UPPER2], F32R)
        w3_sb = sb("w3_sb", [P, M2], F32)
        b1_sb = sb("b1_sb", [P, M1], F32)
        b2_sb = sb("b2_sb", [P, M2], F32)
        eye_sb = sb("eye_sb", [P, P], F32)
        rown_sb = sb("rown_sb", [P, CHUNKS], F32)
        table_hi = sb("table_hi", [P, NL, CHUNKS, P], F32R)
        table_lo = sb("table_lo", [P, NL, CHUNKS, P], F32R)

        idx = [sb(f"idx{u}", [P, FEATURES], I32) for u in range(SUBS)]
        spread = sb("spread", [P, NL, TILE], I32)
        onehot = sb("onehot", [P, RING, CHUNKS, TILE], F32R)
        rows = [sb(f"rows{u}", [P, NG + 1, P], F32) for u in range(SUBS)]
        vectors = sb("vectors", [P, TILE, SLOT], F32)
        x_hi = sb("x_hi", [P, TILE], F32R)
        x_lo = sb("x_lo", [P, TILE], F32R)
        pairs_hi = sb("pairs_hi", [P, JJ, TILE], F32R)
        pairs_lo = sb("pairs_lo", [P, JJ, TILE], F32R)
        r1_hi = sb("r1_hi", [P, M1, TILE], F32R)
        r1_lo = sb("r1_lo", [P, M1, TILE], F32R)

        work = sb("work", [P, SUBS * JJ * P + (M1 + M2 + 1) * TILE], F32)
        at = SUBS * JJ * P
        pairs = [work[:, u * JJ * P:(u + 1) * JJ * P].rearrange("p (k s) -> p k s", k=JJ)
                 for u in range(SUBS)]
        r1 = work[:, at:at + M1 * TILE].rearrange("p (m s) -> p m s", m=M1)
        r2 = work[:, at + M1 * TILE:at + (M1 + M2) * TILE].rearrange("p (m s) -> p m s", m=M2)
        y = work[0:1, at + (M1 + M2) * TILE:at + (M1 + M2 + 1) * TILE]
        w1_raw = work[:, 0:JJ * UPPER1].rearrange("p (k n) -> p k n", k=JJ)

        stage = vectors[:].rearrange("p s v -> p (s v)")
        one = CHUNKS * P
        in_vectors = [stage[:, i * one:(i + 1) * one] for i in range(2)]
        in_rows = [rows[1][:].rearrange("p v d -> p (v d)")[:, i * one:(i + 1) * one] for i in range(2)]
        in_work = [work[:, i * one:(i + 1) * one] for i in range(NL - 4)]
        table_raw = [x.rearrange("p (c d) -> p c d", c=CHUNKS) for x in in_vectors + in_rows + in_work]

        ps_v = [psum(f"ps_v{b}", [P, 512]) for b in range(2)]
        ps_g = [psum(f"ps_g{b}", [P, BQ, P]) for b in range(2)]
        ps_h = [psum(f"ps_h{b}", [P, 512]) for b in range(2)]

        rown_in = sem("rown_in")
        eye_in = sem("eye_in")
        table_in = [sem(f"table_in{l}") for l in range(NL)]
        small_weights_in = sem("small_weights_in")
        w1_in = sem("w1_in")
        rounded = sem("rounded")
        summed = sem("summed")
        table_split = sem("table_split")
        work_free = sem("work_free")
        weights_split = sem("weights_split")
        w1_split = sem("w1_split")
        pads_zeroed = sem("pads_zeroed")
        idx_in = [sem(f"idx_in{u}") for u in range(SUBS)]
        dense_in = [sem(f"dense_in{u}") for u in range(SUBS)]
        rows_in = [[sem(f"rows_in{u}_{g}") for g in range(GB)] for u in range(SUBS)]
        rows_used = [sem(f"rows_used{u}") for u in range(SUBS)]
        gathering = sem("gathering")
        spread_in = sem("spread_in")
        onehot_made = sem("onehot_made")
        onehot_used = sem("onehot_used")
        turned = [sem(f"turned{b}") for b in range(2)]
        vectors_out = [sem(f"vectors_out{b}") for b in range(2)]
        x_hi_out = sem("x_hi_out")
        x_split = sem("x_split")
        products = [sem(f"products{b}") for b in range(2)]
        act_moved = sem("act_moved")
        dve_moved = sem("dve_moved")
        act_group0 = sem("act_group0")
        dve_group0 = sem("dve_group0")
        pairs_hi_out = sem("pairs_hi_out")
        pairs_split = sem("pairs_split")
        layer = [sem(f"layer{b}") for b in range(2)]
        layer_read = [sem(f"layer_read{b}") for b in range(2)]
        r1_split = sem("r1_split")
        stored = sem("stored")
        y_sent = sem("y_sent")

        block = ctx.enter_context(nc.Block())

        @block.sync
        def _(sp):
            def samples(x, n, ahead, u=0, count=TILE):
                return x[ahead * TILE + u * P:, :][bass.ds(n * TILE, count), :]

            def load_spread(n, ahead):
                sp.dma_start(spread[:], looked_ids[:, ahead * TILE:][:, bass.ds(n * TILE, TILE)]
                             .partition_broadcast(P)).then_inc(spread_in, 16)

            def load_idx(n, ahead, u):
                sp.dma_start(idx[u][:], samples(ids, n, ahead, u, P)).then_inc(idx_in[u], 16)

            def load_dense(n, ahead, u):
                sp.dma_start(rows[u][:, NG, :], samples(dense, n, ahead, u, P)).then_inc(dense_in[u], 16)

            def store(n, ahead):
                bank = (STEPS - 1) % 2
                sp.wait_ge(layer_read[bank], n * blocks_in(bank, STEPS)
                           + ((ahead + 1) * blocks_in(bank, STEPS) + FREE))
                sp.dma_start(samples(out, n, ahead).rearrange("b o -> o b"), y).then_inc(stored, 16)
                sp.wait_ge(stored, n * 16 + (ahead + 1) * 16)
                sp.sem_inc(y_sent, 1)

            sp.sem_inc(y_sent, FREE)
            load_idx(0, 0, 0)
            load_spread(0, 0)
            sp.dma_start(rown_sb[:], row_numbers).then_inc(rown_in, 16)
            for l in range(NL):
                sp.dma_start(table_raw[l], small_tables[:, l]).then_inc(table_in[l], 16)
                if l == 1:
                    load_idx(0, 0, 1)
                    sp.dma_start(eye_sb[:], eye).then_inc(eye_in, 16)
                if l == 3:
                    sp.dma_start(wd_raw[:], w1_dense).then_inc(small_weights_in, 16)
                    sp.dma_start(w2_raw[:], w2.rearrange("(k p) n -> p k n", p=P)).then_inc(small_weights_in, 16)
            load_dense(0, 0, 0)
            sp.wait_ge(rows_used[1], FREE)
            load_dense(0, 0, 1)
            sp.wait_ge(work_free, 1)
            sp.dma_start(w1_raw, w1_pairs).then_inc(w1_in, 16)
            def load_next(n, ahead, u):
                for g in range(GB):
                    if gathers(g):
                        sp.wait_ge(rows_in[u][g], n * (16 * gathers(g)) + ahead * (16 * gathers(g)))
                load_idx(n, ahead, u)
                sp.wait_ge(rows_used[u], n + (ahead + FREE))
                load_dense(n, ahead, u)

            def load_next_spread(n, ahead):
                sp.wait_ge(onehot_made, n * (NL * HALVES) + ahead * (NL * HALVES))
                load_spread(n, ahead)

            load_next(0, 1, 0)
            load_next_spread(0, 1)
            load_next(0, 1, 1)
            load_next(0, 2, 0)
            load_next_spread(0, 2)
            store(0, 0)
            load_next(0, 2, 1)
            with sp.Fori(0, tiles - 3) as t:
                load_next(t, 3, 0)
                load_next_spread(t, 3)
                store(t, 1)
                load_next(t, 3, 1)
            store(0, tiles - 2)
            store(0, tiles - 1)

        @block.gpsimd
        def _(pool):
            with pool.Fori(0, tiles) as t:
                for u in range(SUBS):
                    pool.wait_ge(idx_in[u], t * 16 + 16)
                    pool.wait_ge(rows_used[u], t + FREE)
                    pool.sem_inc(gathering, 1)
                    for n, f in enumerate(GATHERED):
                        nc.gpsimd.indirect_dma_start(
                            rows[u][:, n, :], None, tables[f],
                            bass.IndirectOffsetOnAxis(ap=idx[u][:, f:f + 1], axis=0),
                        ).then_inc(rows_in[u][n // 4], 16)

        @block.tensor
        def _(pe):
            def bank_free(t, b):
                pe.wait_ge(vectors_out[bank_of(b)], bank_uses(t, b) + FREE)

            def look_up(t, l):
                b = looked_up_block(l)
                if l % 2 == 0:
                    bank_free(t, b)
                to = ps_v[bank_of(b)][:, (l % 2) * TILE:(l % 2 + 1) * TILE]
                for c in range(CHUNKS):
                    if c % HC == 0:
                        pe.wait_ge(onehot_made, t * (NL * HALVES) + (l * HALVES + c // HC + 1))
                    nc.tensor.matmul(to, table_hi[:, l, c, :], onehot[:, l % RING, c, :], start=c == 0, stop=False)
                    last = nc.tensor.matmul(to, table_lo[:, l, c, :], onehot[:, l % RING, c, :],
                                            start=False, stop=c == CHUNKS - 1)
                    if c % HC == HC - 1:
                        last.then_inc(turned[bank_of(b)] if ends_block(l) and c == CHUNKS - 1 else onehot_used, 1)

            def turn(t, u, some):
                for g in some:
                    if gathers(g):
                        pe.wait_ge(rows_in[u][g], t * (16 * gathers(g)) + 16 * gathers(g))
                    if g == GB - 1:
                        pe.wait_ge(dense_in[u], t * 16 + 16)
                    b = gathered_block(u, g)
                    bank_free(t, b)
                    for n, v in enumerate(gathered_vectors(g)):
                        last = nc.tensor.transpose(ps_v[bank_of(b)][:, n * P:(n + 1) * P],
                                                   rows[u][:, v, :], eye_sb[:])
                    last.then_inc(turned[bank_of(b)], 1)

            def vectors_ready(t, u):
                ready = gathered_block(u + 1, 0)
                for bank in range(2):
                    pe.wait_ge(vectors_out[bank], t * blocks_in(bank) + (blocks_in(bank, ready) + FREE))

            def multiply_pairs(t, u, k):
                before = t * (SUBS * BATCHES) + (u * BATCHES + k - 1 + BANKS)
                pe.wait_ge(act_moved, before)
                pe.wait_ge(dve_moved, before)
                for q in range(BQ):
                    s = u * P + (k * BQ + q) * QUAD
                    last = nc.tensor.matmul(
                        ps_g[k % 2][:, q, 0:QUAD * MOVING],
                        vectors[:, s:s + QUAD, :].rearrange("p s v -> p (s v)"),
                        vectors[:, s:s + QUAD, VECTORS - MOVING:VECTORS], start=True, stop=True)
                last.then_inc(products[k % 2], 1)

            def step_free(t, step):
                pe.wait_ge(layer_read[step % 2], t * blocks_in(step % 2, STEPS) + (step // 2 + FREE))

            def three(step, w_hi, w_lo, a_hi, a_lo, first=False, last=False):
                to = ps_h[step % 2][:, 0:TILE]
                nc.tensor.matmul(to, w_hi, a_hi, start=first, stop=False)
                nc.tensor.matmul(to, w_lo, a_hi, start=False, stop=False)
                return nc.tensor.matmul(to, w_hi, a_lo, start=False, stop=last)

            def layer1(t, m):
                step_free(t, m)
                if m == 0:
                    pe.wait_ge(x_split, t * SUBS + SUBS)
                c = slice(m * P, m * P + P)
                three(m, wd_hi[:, c], wd_lo[:, c], x_hi[:], x_lo[:], first=True)
                if m == 0:
                    pe.wait_ge(pairs_split, t * (SUBS * 2) + SUBS * 2)
                for k in range(JJ):
                    last = three(m, w1_hi[:, k, c], w1_lo[:, k, c], pairs_hi[:, k, :], pairs_lo[:, k, :],
                                 last=k == JJ - 1)
                last.then_inc(layer[m % 2], 1)

            def layer2(t, m):
                step_free(t, M1 + m)
                c = slice(m * P, m * P + P)
                for k in range(M1):
                    if m == 0:
                        pe.wait_ge(r1_split, t * M1 + (k + 1))
                    last = three(M1 + m, w2_hi[:, k, c], w2_lo[:, k, c], r1_hi[:, k, :], r1_lo[:, k, :],
                                 first=k == 0, last=k == M1 - 1)
                last.then_inc(layer[(M1 + m) % 2], 1)

            def layer3(t):
                bank = (M1 + M2) % 2
                step_free(t, M1 + M2)
                for m in range(M2):
                    step = M1 + m
                    pe.wait_ge(layer_read[step % 2], t * blocks_in(step % 2, STEPS) + (step // 2 + 1 + FREE))
                    last = nc.tensor.matmul(ps_h[bank][0:1, 0:TILE], w3_sb[:, m:m + 1], r2[:, m, :],
                                            start=m == 0, stop=m == M2 - 1)
                last.then_inc(layer[bank], 1)

            for l in range(NL):
                pe.wait_ge(table_split, l + 1)
                look_up(0, l)
            pe.wait_ge(eye_in, 16)
            turn(0, 0, range(GB))
            pe.wait_ge(pads_zeroed, 1)
            vectors_ready(0, 0)
            for k in range(BATCHES):
                multiply_pairs(0, 0, k)
            turn(0, 1, range(GB))
            pe.wait_ge(weights_split, 1)
            with pe.Fori(0, tiles - 1) as t:
                vectors_ready(t, 1)
                for k in range(BATCHES):
                    multiply_pairs(t, 1, k)
                look_up(t + 1, 0)
                look_up(t + 1, 1)
                for m in range(M1):
                    layer1(t, m)
                    look_up(t + 1, 2 + m)
                for n in range(3):
                    turn(t + 1, 0, TURNED_AFTER_STEP[n])
                    layer2(t, n) if n < M2 else layer3(t)
                vectors_ready(t + 1, 0)
                for k in range(BATCHES):
                    multiply_pairs(t + 1, 0, k)
                    turn(t + 1, 1, TURNED_AFTER_BATCH[k])
            vectors_ready(tiles - 1, 1)
            for k in range(BATCHES):
                multiply_pairs(tiles - 1, 1, k)
            for m in range(M1):
                layer1(tiles - 1, m)
            for m in range(M2):
                layer2(tiles - 1, m)
            layer3(tiles - 1)

        def block_places(b):
            bank = ps_v[bank_of(b)]
            if b < LB:
                n = min(2, NL - 2 * b)
                return (bank[:, 0:n * TILE].rearrange("p (v s) -> p v s", v=n),
                        vectors[:, :, 2 * b:2 * b + n].rearrange("p s v -> p v s"))
            u, g = divmod(b - LB, GB)
            n, first = len(gathered_vectors(g)), NL + 4 * g
            return (bank[:, 0:n * P].rearrange("p (v s) -> p v s", v=n),
                    vectors[:, u * P:(u + 1) * P, first:first + n].rearrange("p s v -> p v s"))

        def second_place(b):
            n = min(TWICE - 2 * b, 2)
            if n > 0:
                return (ps_v[bank_of(b)][:, 0:n * TILE].rearrange("p (v s) -> p v s", v=n),
                        vectors[:, :, SECOND + 2 * b:SECOND + 2 * b + n].rearrange("p s v -> p v s"))

        def column(s, j):
            return s * MOVING + j - (VECTORS - MOVING)

        def samples_of(k, s):
            first = k * BQ * QUAD + s
            return slice(first, first + (BQ - 1) * QUAD + 1, QUAD)

        def share(u, k, s, g):
            frm = ps_g[k % 2][SLOT * s:SLOT * s + SLOT, :, column(s, TWICE + g):column(s + 1, 1):GROUPS]
            return pairs[u][SLOT * g:SLOT * g + SLOT, :, samples_of(k, s)], frm.rearrange("p q j -> p j q")

        def share_of_first(u, k, s):
            frm = ps_g[k % 2][SLOT * s:SLOT * s + TWICE, :, column(s, 1):column(s, TWICE)]
            return pairs[u][0:TWICE, 0:TWICE - 1, samples_of(k, s)], frm.rearrange("p q j -> p j q")

        @block.scalar
        def _(act):
            def block_out(t, b):
                if bank_of(b) == 0:
                    act.wait_ge(turned[0], bank_uses(t, b) + 1)
                    if b in LAST_OF_ROWS:
                        act.sem_inc(rows_used[LAST_OF_ROWS.index(b)], 1)
                    if second_place(b):
                        frm, to = second_place(b)
                        nc.scalar.copy(to, frm)
                    frm, to = block_places(b)
                    nc.scalar.copy(to, frm).then_inc(vectors_out[0], 1)

            def dense_out(t, u):
                b = gathered_block(u, GB - 1)
                act.wait_ge(vectors_out[bank_of(b)], bank_uses(t, b) + (1 + FREE))
                nc.scalar.copy(x_hi[:, u * P:(u + 1) * P], vectors[:, u * P:(u + 1) * P, VECTORS - 1]
                               ).then_inc(x_hi_out, 1)

            def move(t, u, k):
                act.wait_ge(products[k % 2], t * (SUBS * 2) + (u * 2 + k // 2 + 1))
                for g in range(GROUPS):
                    for s in ACT_SAMPLES:
                        last = nc.scalar.copy(*share(u, k, s, g))
                    if g == 0:
                        last.then_inc(act_group0, 1)
                act.wait_ge(act_group0, t * (SUBS * BATCHES) + (u * BATCHES + k + 1))
                for s in ACT_SAMPLES:
                    last = nc.scalar.copy(*share_of_first(u, k, s))
                last.then_inc(act_moved, 1)

            def round_pairs(t, u, h):
                moved = u * BATCHES + (h + 1) * BATCHES // 2 + BANKS
                act.wait_ge(act_moved, t * (SUBS * BATCHES) + moved)
                act.wait_ge(dve_moved, t * (SUBS * BATCHES) + moved)
                a, b = h * P // 2, (h + 1) * P // 2
                nc.scalar.copy(pairs_hi[:, :, u * P + a:u * P + b], pairs[u][:, :, a:b]).then_inc(pairs_hi_out, 1)

            def layer_out(t, step):
                bank = step % 2
                act.wait_ge(layer[bank], t * blocks_in(bank, STEPS) + (step // 2 + 1))
                frm = ps_h[bank][:, 0:TILE]
                if step < M1:
                    bias = b1_sb[:, step:step + 1]
                    nc.scalar.activation(r1[:, step, :], frm, ACT.Relu, bias=bias)
                    last = nc.scalar.activation(r1_hi[:, step, :], frm, ACT.Relu, bias=bias)
                elif step < M1 + M2:
                    m = step - M1
                    last = nc.scalar.activation(r2[:, m, :], frm, ACT.Relu, bias=b2_sb[:, m:m + 1])
                else:
                    act.wait_ge(y_sent, t + FREE)
                    last = nc.scalar.copy(y, ps_h[bank][0:1, 0:TILE])
                last.then_inc(layer_read[bank], 1)

            act.sem_inc(rows_used[0], FREE)
            act.sem_inc(vectors_out[0], FREE)
            act.sem_inc(act_moved, BANKS)
            for bank in range(2):
                act.sem_inc(layer_read[bank], FREE)
            act.dma_start(w3_sb[:], w3).then_inc(small_weights_in, 16)
            act.dma_start(b1_sb[:], b1).then_inc(small_weights_in, 16)
            act.dma_start(b2_sb[:], b2).then_inc(small_weights_in, 16)
            for l in range(NL):
                act.wait_ge(table_in[l], 16)
                nc.scalar.copy(table_hi[:, l], table_raw[l]).then_inc(rounded, 1)
                if l == 1:
                    act.wait_ge(table_split, 2)
                if l == NL - 1:
                    block_out(0, looked_up_block(0))
            act.wait_ge(small_weights_in, 16 * 5)
            nc.scalar.copy(w2_hi[:], w2_raw[:]).then_inc(rounded, 1)
            block_out(0, looked_up_block(4))
            act.wait_ge(w1_in, 16)
            nc.scalar.copy(w1_hi[:], w1_raw).then_inc(rounded, 1)
            for g in range(GB):
                block_out(0, gathered_block(0, g))
            dense_out(0, 0)
            act.wait_ge(summed, 1)
            nc.scalar.copy(wd_hi[:], wd_sum[:]).then_inc(rounded, 1)
            act.wait_ge(w1_split, 1)
            for k in range(BATCHES):
                move(0, 0, k)
                if k % 2:
                    round_pairs(0, 0, k // 2)
            for g in range(GB):
                block_out(0, gathered_block(1, g))
            dense_out(0, 1)
            with act.Fori(0, tiles - 1) as t:
                for k in range(BATCHES):
                    move(t, 1, k)
                    if k % 2:
                        round_pairs(t, 1, k // 2)
                for m in range(M1):
                    if m % 2 == 0:
                        block_out(t + 1, m // 2)
                    layer_out(t, m)
                block_out(t + 1, LB - 1)
                for n in range(3):
                    for g in TURNED_AFTER_STEP[n]:
                        block_out(t + 1, gathered_block(0, g))
                    layer_out(t, M1 + n)
                dense_out(t + 1, 0)
                for k in range(BATCHES):
                    move(t + 1, 0, k)
                    if k % 2:
                        round_pairs(t + 1, 0, k // 2)
                    for g in TURNED_AFTER_BATCH[k]:
                        block_out(t + 1, gathered_block(1, g))
                dense_out(t + 1, 1)
            for k in range(BATCHES):
                move(tiles - 1, 1, k)
                if k % 2:
                    round_pairs(tiles - 1, 1, k // 2)
            for step in range(STEPS):
                layer_out(tiles - 1, step)

        @block.vector
        def _(dve):
            def half_used(t, l, h):
                if ends_block(l) and h == HALVES - 1:
                    b = looked_up_block(l)
                    dve.wait_ge(turned[bank_of(b)], bank_uses(t, b) + 1)
                else:
                    dve.wait_ge(onehot_used, t * (NL * HALVES - LB) + (l * HALVES - l // 2 + h + 1))

            def make_onehot(t, l, halves=range(HALVES), first=False):
                for h in halves:
                    if l >= RING:
                        half_used(t, l - RING, h)
                    elif not first:
                        half_used(t - 1, max(i for i in range(NL) if i % RING == l), h)
                    for c in range(h * HC, (h + 1) * HC):
                        last = nc.vector.tensor_scalar(onehot[:, l % RING, c, :], spread[:, l, :], rown_sb[:, c:c + 1],
                                                       None, ALU.is_equal)
                    last.then_inc(onehot_made, 1)

            def block_out(t, b):
                if bank_of(b) == 1:
                    dve.wait_ge(turned[1], bank_uses(t, b) + 1)
                    if b in LAST_OF_ROWS:
                        dve.sem_inc(rows_used[LAST_OF_ROWS.index(b)], 1)
                    if second_place(b):
                        frm, to = second_place(b)
                        nc.vector.tensor_copy(to, frm)
                    frm, to = block_places(b)
                    nc.vector.tensor_copy(to, frm).then_inc(vectors_out[1], 1)

            def dense_out(t, u):
                dve.wait_ge(x_hi_out, t * SUBS + (u + 1))
                nc.vector.tensor_tensor(x_lo[:, u * P:(u + 1) * P], vectors[:, u * P:(u + 1) * P, VECTORS - 1],
                                        x_hi[:, u * P:(u + 1) * P].bitcast(F32), ALU.subtract).then_inc(x_split, 1)

            def move(t, u, k):
                dve.wait_ge(products[k % 2], t * (SUBS * 2) + (u * 2 + k // 2 + 1))
                for g in range(GROUPS):
                    for s in DVE_SAMPLES:
                        last = nc.vector.tensor_copy(*share(u, k, s, g))
                    if g == 0:
                        last.then_inc(dve_group0, 1)
                dve.wait_ge(dve_group0, t * (SUBS * BATCHES) + (u * BATCHES + k + 1))
                for s in DVE_SAMPLES:
                    last = nc.vector.tensor_copy(*share_of_first(u, k, s))
                last.then_inc(dve_moved, 1)

            def split_pairs(t, u, h):
                dve.wait_ge(pairs_hi_out, t * (SUBS * 2) + (u * 2 + h + 1))
                a, b = h * P // 2, (h + 1) * P // 2
                nc.vector.tensor_tensor(pairs_lo[:, :, u * P + a:u * P + b], pairs[u][:, :, a:b],
                                        pairs_hi[:, :, u * P + a:u * P + b].bitcast(F32), ALU.subtract
                                        ).then_inc(pairs_split, 1)

            def split_r1(t, m):
                dve.wait_ge(layer_read[m % 2], t * blocks_in(m % 2, STEPS) + (m // 2 + 1 + FREE))
                nc.vector.tensor_tensor(r1_lo[:, m, :], r1[:, m, :], r1_hi[:, m, :].bitcast(F32),
                                        ALU.subtract).then_inc(r1_split, 1)

            dve.sem_inc(vectors_out[1], FREE)
            dve.sem_inc(dve_moved, BANKS)
            def split_table(l, done):
                dve.wait_ge(rounded, done)
                nc.vector.tensor_tensor(table_lo[:, l], table_raw[l], table_hi[:, l].bitcast(F32),
                                        ALU.subtract).then_inc(table_split, 1)

            dve.wait_ge(rown_in, 16)
            dve.wait_ge(spread_in, 16)
            make_onehot(0, 0, first=True)
            split_table(0, 1)
            split_table(1, 2)
            make_onehot(0, 1, first=True)
            split_table(2, 3)
            make_onehot(0, 2)
            split_table(3, 4)
            dve.wait_ge(table_split, 4)
            dve.sem_inc(rows_used[1], FREE)
            make_onehot(0, 3)
            split_table(4, 5)
            make_onehot(0, 4)
            split_table(5, 6)
            dve.wait_ge(table_split, 6)
            dve.sem_inc(work_free, 1)
            make_onehot(0, 5)
            block_out(0, 1)
            for g in range(GB):
                block_out(0, gathered_block(0, g))
                if g == 1:
                    nc.vector.memset(vectors[:, :, SECOND + TWICE:SLOT], 0.0).then_inc(pads_zeroed, 1)
            dve.wait_ge(small_weights_in, 16 * 5)
            nc.vector.tensor_tensor(wd_sum[:], wd_raw[:, 0, :], wd_raw[:, 1, :], ALU.add).then_inc(summed, 1)
            dve.wait_ge(rounded, NL + 2)
            nc.vector.tensor_tensor(w1_lo[:], w1_raw, w1_hi[:].bitcast(F32), ALU.subtract).then_inc(w1_split, 1)
            dve.wait_ge(w1_split, 1)
            dense_out(0, 0)
            for k in range(BATCHES):
                move(0, 0, k)
                if k % 2:
                    split_pairs(0, 0, k // 2)
            nc.vector.tensor_tensor(w2_lo[:], w2_raw[:], w2_hi[:].bitcast(F32), ALU.subtract)
            dve.wait_ge(rounded, NL + 3)
            nc.vector.tensor_tensor(wd_lo[:], wd_sum[:], wd_hi[:].bitcast(F32), ALU.subtract).then_inc(weights_split, 1)
            for g in range(GB):
                block_out(0, gathered_block(1, g))
            dense_out(0, 1)
            with dve.Fori(0, tiles - 1) as t:
                dve.wait_ge(spread_in, t * 16 + 32)
                for k in range(BATCHES):
                    move(t, 1, k)
                    if k == 2:
                        split_pairs(t, 1, 0)
                    make_onehot(t + 1, k // HALVES, [k % HALVES])
                split_pairs(t, 1, 1)
                for m in range(M1):
                    make_onehot(t + 1, 2 + m)
                    split_r1(t, m)
                    if m == 2:
                        block_out(t + 1, 1)
                for g in sum(TURNED_AFTER_STEP, []):
                    block_out(t + 1, gathered_block(0, g))
                dense_out(t + 1, 0)
                for k in range(BATCHES):
                    move(t + 1, 0, k)
                    if k == 2:
                        split_pairs(t + 1, 0, 0)
                    for g in TURNED_AFTER_BATCH[k]:
                        block_out(t + 1, gathered_block(1, g))
                split_pairs(t + 1, 0, 1)
                dense_out(t + 1, 1)
            for k in range(BATCHES):
                move(tiles - 1, 1, k)
                if k % 2:
                    split_pairs(tiles - 1, 1, k // 2)
            for m in range(M1):
                split_r1(tiles - 1, m)



def pair_rows():
    row = {}
    at = P + FEATURES
    for i in range(FEATURES):
        row[i, FEATURES] = P + i
        for j in range(i + 1, FEATURES):
            row[i, j] = at
            at += 1

    def row_of(i, j):
        return row[min(ORDER[i], ORDER[j]), max(ORDER[i], ORDER[j])]

    where = np.full((JJ, GROUPS, SLOT), -1)
    for j in range(TWICE, VECTORS):
        for i in range(j):
            where[(j - TWICE) // GROUPS, (j - TWICE) % GROUPS, i if i >= TWICE else SECOND + i] = row_of(i, j)
    for j in range(1, TWICE):
        for i in range(j):
            where[j - 1, 0, i] = row_of(i, j)
    return where.reshape(JJ, P)


def kernel(**inputs):
    import concourse.bacc as bacc
    from concourse.bass_utils import run_bass_kernel_spmd

    a = {k: np.asarray(v) for k, v in inputs.items()}
    where = pair_rows()
    w1 = a["W_top1"]
    w1_pairs = np.zeros((JJ, P, UPPER1), w1.dtype)
    w1_pairs[where >= 0] = w1[where[where >= 0]]
    small = np.zeros((NL, CHUNKS * P, P), np.float32)
    for l, f in enumerate(LOOKED_UP):
        small[l, :len(a[f"tbl_{f}"])] = a[f"tbl_{f}"]
    data = {
        "ids": a["ids"],
        "looked_ids": np.ascontiguousarray(a["ids"][:, LOOKED_UP].T),
        "dense": a["r_dense_features"],
        "small_tables": np.ascontiguousarray(small.reshape(NL, CHUNKS, P, P).transpose(2, 0, 1, 3)),
        "w1_pairs": np.ascontiguousarray(w1_pairs.transpose(1, 0, 2)),
        "w1_dense": np.stack([w1[:P], w1[-P:]], axis=1),
        "b1": np.ascontiguousarray(a["b_top1"].reshape(M1, P).T),
        "w2": a["W_top2"],
        "b2": np.ascontiguousarray(a["b_top2"].reshape(M2, P).T),
        "w3": np.ascontiguousarray(a["W_top3"].reshape(M2, P).T),
        "eye": np.eye(P, dtype=np.float32),
        "row_numbers": np.arange(CHUNKS * P, dtype=np.float32).reshape(CHUNKS, P).T.copy(),
    }
    for f in GATHERED:
        data[f"tbl_{f}"] = a[f"tbl_{f}"]
    nc = bacc.Bacc("TRN2", target_bir_lowering=False, num_devices=1)
    d = {k: nc.dram_tensor(f"in_{k}", v.shape, mybir.dt.from_np(v.dtype), kind="ExternalInput").ap()
         for k, v in data.items()}
    out = nc.dram_tensor("out_y", (a["ids"].shape[0], 1), F32, kind="ExternalOutput").ap()
    build_dlrm_tower(nc, d["ids"], d["looked_ids"], d["dense"], {f: d[f"tbl_{f}"] for f in GATHERED}, d["small_tables"],
                     d["w1_pairs"], d["w1_dense"], d["b1"], d["w2"], d["b2"], d["w3"], d["eye"],
                     d["row_numbers"], out)
    r = run_bass_kernel_spmd(nc, [{f"in_{k}": v for k, v in data.items()}], core_ids=[0])
    return r.results[0]["out_y"]
```

```python
from contextlib import ExitStack

import numpy as np

import concourse.bass as bass
from concourse import mybir

ALU = mybir.AluOpType
ACT = mybir.ActivationFunctionType
F32 = mybir.dt.float32
F32R = mybir.dt.float32r
I32 = mybir.dt.int32

P = 128
FEATURES = 26
VECTORS = FEATURES + 1
SLOT = 32
QUAD = P // SLOT
TWICE = 3
SECOND = VECTORS
GROUPS = P // SLOT
JJ = (VECTORS - TWICE) // GROUPS
MOVING = VECTORS - 1
SUBS = 2
TILE = SUBS * P
BATCHES = 4
BQ = P // QUAD // BATCHES
UPPER1, UPPER2 = 512, 256
M1, M2 = UPPER1 // P, UPPER2 // P

LOOKED_UP = [2, 4, 6, 7, 8, 10]
GATHERED = [f for f in range(FEATURES) if f not in LOOKED_UP]
ORDER = LOOKED_UP + GATHERED + [FEATURES]
NL, NG = len(LOOKED_UP), len(GATHERED)
CHUNKS = 8
HALVES = 2
HC = CHUNKS // HALVES
RING = 2

LB = -(-NL // 2)
GB = -(-NG // 4)
BLOCKS = LB + SUBS * GB

TURNED_AFTER_STEP = {2: [(0, 0)], 3: [(0, 1), (0, 2)], 4: [(0, 3), (0, 4)], 5: [(1, 0), (1, 1)]}
TURNED_AFTER_BATCH = [[], [(1, 2), (1, 3)], [(1, 4)], []]
LOOKED_UP_AFTER_STEP = {0: [2], 1: [3], 2: [4, 5]}

ACT_SAMPLES, DVE_SAMPLES = (0, 1, 2), (3,)
LAST_ACT_SAMPLES, LAST_DVE_SAMPLES = (0, 1), (2, 3)

FREE = 1
BANKS = 2


def gathered_block(u, g):
    return LB + u * GB + g


def looked_up_block(l):
    return l // 2


def ends_block(l):
    return l % 2 == 1 or l == NL - 1


BEFORE_PRODUCTS = sum(TURNED_AFTER_STEP.values(), [])
ALL_TURNED = BEFORE_PRODUCTS + sum(TURNED_AFTER_BATCH, [])

LAST_OF_ROWS = [[gathered_block(v, g) for v, g in ALL_TURNED if v == u][-1] for u in range(SUBS)]


def bank_of(block):
    return block % 2


def blocks_in(bank, blocks=BLOCKS):
    return (blocks - bank + 1) // 2


def bank_uses(t, block):
    return t * blocks_in(bank_of(block)) + blocks_in(bank_of(block), block)


def gathers(g):
    return range(4 * g, min(4 * g + 4, NG))


STEPS = M1 + M2 + 1


def build_dlrm_tower(nc, ids, looked_ids, dense, tables, small_tables, w1_pairs, w1_dense, b1, w2, b2, w3, eye,
                     row_numbers, out):
    tiles = ids.shape[0] // TILE
    ctx = ExitStack()
    with ctx:
        def sb(name, shape, dt):
            return ctx.enter_context(nc.sbuf_tensor(name, shape, dt))

        def psum(name, shape):
            return ctx.enter_context(nc.psum_tensor(name, shape, F32))

        def sem(name):
            return ctx.enter_context(nc.semaphore(name))

        w1_hi = sb("w1_hi", [P, JJ, UPPER1], F32R)
        w1_lo = sb("w1_lo", [P, JJ, UPPER1], F32R)
        wd_raw = sb("wd_raw", [P, 2, UPPER1], F32)
        w2_raw = sb("w2_raw", [P, M1, UPPER2], F32)
        wd_sum = sb("wd_sum", [P, UPPER1], F32)
        wd_hi = sb("wd_hi", [P, UPPER1], F32R)
        wd_lo = sb("wd_lo", [P, UPPER1], F32R)
        w2_hi = sb("w2_hi", [P, M1, UPPER2], F32R)
        w2_lo = sb("w2_lo", [P, M1, UPPER2], F32R)
        w3_sb = sb("w3_sb", [P, M2], F32)
        ones = sb("ones", [P, 1], F32)
        b1_sb = sb("b1_sb", [P, M1], F32)
        b2_sb = sb("b2_sb", [P, M2], F32)
        eye_sb = sb("eye_sb", [P, P], F32)
        rown_sb = sb("rown_sb", [P, CHUNKS], F32)
        table_hi = sb("table_hi", [P, NL, CHUNKS, P], F32R)
        table_lo = sb("table_lo", [P, NL, CHUNKS, P], F32R)

        idx = [sb(f"idx{u}", [P, FEATURES], I32) for u in range(SUBS)]
        spread = sb("spread", [P, NL, TILE], I32)
        onehot = sb("onehot", [P, RING, CHUNKS, TILE], F32R)
        rows = [sb(f"rows{u}", [P, NG, P], F32) for u in range(SUBS)]
        vectors = sb("vectors", [P, TILE, SLOT], F32)
        x = sb("x", [P, TILE], F32)
        x_hi = sb("x_hi", [P, TILE], F32R)
        x_lo = sb("x_lo", [P, TILE], F32R)
        pairs_hi = sb("pairs_hi", [P, JJ, TILE], F32R)
        pairs_lo = sb("pairs_lo", [P, JJ, TILE], F32R)
        r1_hi = sb("r1_hi", [P, M1, TILE], F32R)
        r1_lo = sb("r1_lo", [P, M1, TILE], F32R)

        work = sb("work", [P, SUBS * JJ * P + (M1 + M2 + 3) * TILE], F32)
        at = SUBS * JJ * P
        pairs = [work[:, u * JJ * P:(u + 1) * JJ * P].rearrange("p (k s) -> p k s", k=JJ)
                 for u in range(SUBS)]
        r1 = work[:, at:at + M1 * TILE].rearrange("p (m s) -> p m s", m=M1)
        r2 = work[:, at + M1 * TILE:at + (M1 + M2) * TILE].rearrange("p (m s) -> p m s", m=M2)
        weighted = work[:, at + (M1 + M2) * TILE:at + (M1 + M2 + 2) * TILE].rearrange("p (m s) -> p m s", m=2)
        y = work[0:1, at + (M1 + M2 + 2) * TILE:at + (M1 + M2 + 3) * TILE]

        w1_raw = work[:, 0:JJ * UPPER1].rearrange("p (k n) -> p k n", k=JJ)
        one = CHUNKS * P
        tables_in_vectors = NL - NG * P // one
        flat_vectors, flat_rows = vectors[:].rearrange("p s v -> p (s v)"), rows[1][:].rearrange("p v d -> p (v d)")
        places = [flat_vectors[:, i * one:(i + 1) * one] for i in range(tables_in_vectors)]
        places += [flat_rows[:, i * one:(i + 1) * one] for i in range(NL - tables_in_vectors)]
        table_raw = [place.rearrange("p (c d) -> p c d", c=CHUNKS) for place in places]

        ps_v = [psum(f"ps_v{b}", [P, 512]) for b in range(2)]
        ps_g = [psum(f"ps_g{b}", [P, BQ, P]) for b in range(2)]
        ps_h = [psum(f"ps_h{b}", [P, 512]) for b in range(2)]

        rown_in = sem("rown_in")
        eye_in = sem("eye_in")
        table_in = [sem(f"table_in{l}") for l in range(NL)]
        small_weights_in = sem("small_weights_in")
        w1_in = sem("w1_in")
        rounded = sem("rounded")
        summed = sem("summed")
        table_split = sem("table_split")
        weights_split = sem("weights_split")
        w1_split = sem("w1_split")
        pads_zeroed = sem("pads_zeroed")
        idx_in = [sem(f"idx_in{u}") for u in range(SUBS)]
        dense_in = sem("dense_in")
        rows_in = [[sem(f"rows_in{u}_{g}") for g in range(GB)] for u in range(SUBS)]
        rows_used = [sem(f"rows_used{u}") for u in range(SUBS)]
        gathering = sem("gathering")
        spread_in = sem("spread_in")
        onehot_made = sem("onehot_made")
        onehot_used = sem("onehot_used")
        turned = [sem(f"turned{b}") for b in range(2)]
        vectors_out = [sem(f"vectors_out{b}") for b in range(2)]
        x_hi_out = sem("x_hi_out")
        x_split = sem("x_split")
        products = [sem(f"products{b}") for b in range(2)]
        act_moved = sem("act_moved")
        dve_moved = sem("dve_moved")
        act_group0 = sem("act_group0")
        dve_group0 = sem("dve_group0")
        pairs_hi_out = sem("pairs_hi_out")
        pairs_split = sem("pairs_split")
        layer = [sem(f"layer{b}") for b in range(2)]
        layer_read = [sem(f"layer_read{b}") for b in range(2)]
        r1_split = sem("r1_split")
        r2_weighted = sem("r2_weighted")
        stored = sem("stored")
        y_sent = sem("y_sent")

        block = ctx.enter_context(nc.Block())

        @block.sync
        def _(sp):
            def samples(a, n, ahead, u=0, count=TILE):
                return a[ahead * TILE + u * P:, :][bass.ds(n * TILE, count), :]

            def load_spread(n, ahead):
                sp.dma_start(spread[:], looked_ids[:, ahead * TILE:][:, bass.ds(n * TILE, TILE)]
                             .partition_broadcast(P)).then_inc(spread_in, 16)

            def load_idx(n, ahead, u):
                sp.dma_start(idx[u][:], samples(ids, n, ahead, u, P)).then_inc(idx_in[u], 16)

            def load_dense(n, ahead):
                sp.dma_start(x[:], dense[:, ahead * TILE:][:, bass.ds(n * TILE, TILE)]).then_inc(dense_in, 16)

            def store(n, ahead):
                bank = (STEPS - 1) % 2
                sp.wait_ge(layer_read[bank], n * blocks_in(bank, STEPS)
                           + ((ahead + 1) * blocks_in(bank, STEPS) + FREE))
                sp.dma_start(samples(out, n, ahead).rearrange("b o -> o b"), y).then_inc(stored, 16)
                sp.wait_ge(stored, n * 16 + (ahead + 1) * 16)
                sp.sem_inc(y_sent, 1)

            sp.sem_inc(y_sent, FREE)
            load_idx(0, 0, 0)
            load_spread(0, 0)
            sp.dma_start(rown_sb[:], row_numbers).then_inc(rown_in, 16)
            for l in range(NL):
                sp.dma_start(table_raw[l], small_tables[:, l]).then_inc(table_in[l], 16)
                if l == 1:
                    load_idx(0, 0, 1)
                    sp.dma_start(eye_sb[:], eye).then_inc(eye_in, 16)
                if l == 3:
                    sp.dma_start(wd_raw[:], w1_dense).then_inc(small_weights_in, 16)
                    sp.dma_start(w2_raw[:], w2.rearrange("(k p) n -> p k n", p=P)).then_inc(small_weights_in, 16)
            load_dense(0, 0)
            sp.dma_start(w1_raw, w1_pairs).then_inc(w1_in, 16)

            def load_next(n, ahead, u):
                for g in range(GB):
                    each = 16 * len(gathers(g))
                    sp.wait_ge(rows_in[u][g], n * each + ahead * each)
                load_idx(n, ahead, u)

            def load_next_dense(n, ahead):
                sp.wait_ge(x_split, n + ahead)
                load_dense(n, ahead)

            def load_next_spread(n, ahead):
                sp.wait_ge(onehot_made, n * (NL * HALVES) + ahead * (NL * HALVES))
                load_spread(n, ahead)

            load_next(0, 1, 0)
            load_next_spread(0, 1)
            load_next_dense(0, 1)
            load_next(0, 1, 1)
            load_next(0, 2, 0)
            load_next_spread(0, 2)
            load_next_dense(0, 2)
            store(0, 0)
            load_next(0, 2, 1)
            with sp.Fori(0, tiles - 3) as t:
                load_next(t, 3, 0)
                load_next_spread(t, 3)
                load_next_dense(t, 3)
                store(t, 1)
                load_next(t, 3, 1)
            store(0, tiles - 2)
            store(0, tiles - 1)

        @block.gpsimd
        def _(pool):
            with pool.Fori(0, tiles) as t:
                for u in range(SUBS):
                    pool.wait_ge(idx_in[u], t * 16 + 16)
                    pool.wait_ge(rows_used[u], t + FREE)
                    pool.sem_inc(gathering, 1)
                    for n, f in enumerate(GATHERED):
                        nc.gpsimd.indirect_dma_start(
                            rows[u][:, n, :], None, tables[f],
                            bass.IndirectOffsetOnAxis(ap=idx[u][:, f:f + 1], axis=0),
                        ).then_inc(rows_in[u][n // 4], 16)

        @block.tensor
        def _(pe):
            def bank_free(t, b):
                pe.wait_ge(vectors_out[bank_of(b)], bank_uses(t, b) + FREE)

            def look_up(t, l):
                b = looked_up_block(l)
                if l % 2 == 0:
                    bank_free(t, b)
                to = ps_v[bank_of(b)][:, (l % 2) * TILE:(l % 2 + 1) * TILE]
                for c in range(CHUNKS):
                    if c % HC == 0:
                        pe.wait_ge(onehot_made, t * (NL * HALVES) + (l * HALVES + c // HC + 1))
                    nc.tensor.matmul(to, table_hi[:, l, c, :], onehot[:, l % RING, c, :], start=c == 0, stop=False)
                    last = nc.tensor.matmul(to, table_lo[:, l, c, :], onehot[:, l % RING, c, :],
                                            start=False, stop=c == CHUNKS - 1)
                    if c % HC == HC - 1:
                        last.then_inc(turned[bank_of(b)] if ends_block(l) and c == CHUNKS - 1 else onehot_used, 1)

            def turn(t, some):
                for u, g in some:
                    b = gathered_block(u, g)
                    each = 16 * len(gathers(g))
                    pe.wait_ge(rows_in[u][g], t * each + each)
                    bank_free(t, b)
                    for n, v in enumerate(gathers(g)):
                        last = nc.tensor.transpose(ps_v[bank_of(b)][:, n * P:(n + 1) * P],
                                                   rows[u][:, v, :], eye_sb[:])
                    last.then_inc(turned[bank_of(b)], 1)

            def vectors_ready(t, u):
                pe.wait_ge(x_split, t + 1)
                ready = gathered_block(u + 1, 0)
                for bank in range(2):
                    pe.wait_ge(vectors_out[bank], t * blocks_in(bank) + (blocks_in(bank, ready) + FREE))

            def multiply_pairs(t, u, k):
                before = t * (SUBS * BATCHES) + (u * BATCHES + k - 1 + BANKS)
                pe.wait_ge(act_moved, before)
                pe.wait_ge(dve_moved, before)
                for q in range(BQ):
                    s = u * P + (k * BQ + q) * QUAD
                    last = nc.tensor.matmul(
                        ps_g[k % 2][:, q, 0:QUAD * MOVING],
                        vectors[:, s:s + QUAD, :].rearrange("p s v -> p (s v)"),
                        vectors[:, s:s + QUAD, VECTORS - MOVING:VECTORS], start=True, stop=True)
                last.then_inc(products[k % 2], 1)

            def step_free(t, step):
                pe.wait_ge(layer_read[step % 2], t * blocks_in(step % 2, STEPS) + (step // 2 + FREE))

            def with_high(step, w_hi, w_lo, a_hi, first=False):
                to = ps_h[step % 2][:, 0:TILE]
                nc.tensor.matmul(to, w_hi, a_hi, start=first, stop=False)
                nc.tensor.matmul(to, w_lo, a_hi, start=False, stop=False)

            def with_low(step, w_hi, a_lo, last=False):
                return nc.tensor.matmul(ps_h[step % 2][:, 0:TILE], w_hi, a_lo, start=False, stop=last)

            def layer1_dense(t, m):
                step_free(t, m)
                c = slice(m * P, m * P + P)
                with_high(m, wd_hi[:, c], wd_lo[:, c], x_hi[:], first=True)
                with_low(m, wd_hi[:, c], x_lo[:])

            def layer1_pairs(t, m):
                c = slice(m * P, m * P + P)
                if m == 0:
                    pe.wait_ge(pairs_hi_out, t * (SUBS * 2) + SUBS * 2)
                for k in range(JJ):
                    with_high(m, w1_hi[:, k, c], w1_lo[:, k, c], pairs_hi[:, k, :])
                if m == 0:
                    pe.wait_ge(pairs_split, t * (SUBS * 2) + SUBS * 2)
                for k in range(JJ):
                    last = with_low(m, w1_hi[:, k, c], pairs_lo[:, k, :], last=k == JJ - 1)
                last.then_inc(layer[m % 2], 1)

            def layer1(t, m):
                layer1_dense(t, m)
                layer1_pairs(t, m)

            def layer2(t, m):
                step = M1 + m
                step_free(t, step)
                c = slice(m * P, m * P + P)
                for k in range(M1):
                    if m == 0:
                        pe.wait_ge(layer_read[k % 2], t * blocks_in(k % 2, STEPS) + (k // 2 + 1 + FREE))
                    with_high(step, w2_hi[:, k, c], w2_lo[:, k, c], r1_hi[:, k, :], first=k == 0)
                if m == 0:
                    pe.wait_ge(r1_split, t * M1 + M1)
                for k in range(M1):
                    last = with_low(step, w2_hi[:, k, c], r1_lo[:, k, :], last=k == M1 - 1)
                last.then_inc(layer[step % 2], 1)

            def layer3(t):
                step_free(t, M1 + M2)
                pe.wait_ge(r2_weighted, t * M2 + M2)
                nc.tensor.matmul(ps_h[(M1 + M2) % 2][0:1, 0:TILE], ones[:], weighted[:, M2 - 1, :],
                                 start=True, stop=True).then_inc(layer[(M1 + M2) % 2], 1)

            def multiply_first(t, tower=None):
                vectors_ready(t, 0)
                for k in range(BATCHES):
                    multiply_pairs(t, 0, k)
                    if k == 0 and tower is not None:
                        layer3(tower)
                    turn(t, TURNED_AFTER_BATCH[k])

            def multiply_second(t):
                vectors_ready(t, 1)
                for k in range(BATCHES):
                    multiply_pairs(t, 1, k)

            for l in range(NL):
                pe.wait_ge(table_split, l + 1)
                look_up(0, l)
            pe.wait_ge(eye_in, 16)
            turn(0, BEFORE_PRODUCTS)
            pe.wait_ge(pads_zeroed, 1)
            multiply_first(0)
            with pe.Fori(0, tiles - 1) as t:
                multiply_second(t)
                pe.wait_ge(weights_split, 1)
                look_up(t + 1, 0)
                look_up(t + 1, 1)
                for step in range(M1 + M2):
                    layer1(t, step) if step < M1 else layer2(t, step - M1)
                    for l in LOOKED_UP_AFTER_STEP.get(step, []):
                        look_up(t + 1, l)
                    turn(t + 1, TURNED_AFTER_STEP.get(step, []))
                multiply_first(t + 1, tower=t)
            multiply_second(tiles - 1)
            for m in range(2):
                layer1_dense(tiles - 1, m)
            for m in range(M1):
                if m >= 2:
                    layer1_dense(tiles - 1, m)
                layer1_pairs(tiles - 1, m)
            for m in range(M2):
                layer2(tiles - 1, m)
            layer3(tiles - 1)

        def block_places(b):
            bank = ps_v[bank_of(b)]
            if b < LB:
                n = min(2, NL - 2 * b)
                return (bank[:, 0:n * TILE].rearrange("p (v s) -> p v s", v=n),
                        vectors[:, :, 2 * b:2 * b + n].rearrange("p s v -> p v s"))
            u, g = divmod(b - LB, GB)
            n, first = len(gathers(g)), NL + 4 * g
            return (bank[:, 0:n * P].rearrange("p (v s) -> p v s", v=n),
                    vectors[:, u * P:(u + 1) * P, first:first + n].rearrange("p s v -> p v s"))

        def second_place(b):
            n = min(TWICE - 2 * b, 2)
            if n > 0:
                return (ps_v[bank_of(b)][:, 0:n * TILE].rearrange("p (v s) -> p v s", v=n),
                        vectors[:, :, SECOND + 2 * b:SECOND + 2 * b + n].rearrange("p s v -> p v s"))

        def column(s, j):
            return s * MOVING + j - (VECTORS - MOVING)

        def samples_of(k, s):
            first = k * BQ * QUAD + s
            return slice(first, first + (BQ - 1) * QUAD + 1, QUAD)

        def share(u, k, s, g):
            frm = ps_g[k % 2][SLOT * s:SLOT * s + SLOT, :, column(s, TWICE + g):column(s + 1, 1):GROUPS]
            return pairs[u][SLOT * g:SLOT * g + SLOT, :, samples_of(k, s)], frm.rearrange("p q j -> p j q")

        def share_of_first(u, k, s):
            frm = ps_g[k % 2][SLOT * s:SLOT * s + TWICE, :, column(s, 1):column(s, TWICE)]
            return pairs[u][0:TWICE, 0:TWICE - 1, samples_of(k, s)], frm.rearrange("p q j -> p j q")

        @block.scalar
        def _(act):
            def block_out(t, b):
                if bank_of(b) == 0:
                    act.wait_ge(turned[0], bank_uses(t, b) + 1)
                    if b in LAST_OF_ROWS:
                        act.sem_inc(rows_used[LAST_OF_ROWS.index(b)], 1)
                    if second_place(b):
                        frm, to = second_place(b)
                        nc.scalar.copy(to, frm)
                    frm, to = block_places(b)
                    nc.scalar.copy(to, frm).then_inc(vectors_out[0], 1)

            def dense_out(t):
                act.wait_ge(dense_in, t * 16 + 16)
                nc.scalar.copy(x_hi[:], x[:]).then_inc(x_hi_out, 1)

            def move(t, u, k, samples=ACT_SAMPLES):
                act.wait_ge(products[k % 2], t * (SUBS * 2) + (u * 2 + k // 2 + 1))
                for g in range(GROUPS):
                    for s in samples:
                        last = nc.scalar.copy(*share(u, k, s, g))
                    if g == 0:
                        last.then_inc(act_group0, 1)
                act.wait_ge(act_group0, t * (SUBS * BATCHES) + (u * BATCHES + k + 1))
                for s in samples:
                    last = nc.scalar.copy(*share_of_first(u, k, s))
                last.then_inc(act_moved, 1)

            def round_pairs(t, u, h):
                moved = u * BATCHES + (h + 1) * BATCHES // 2 + BANKS
                act.wait_ge(act_moved, t * (SUBS * BATCHES) + moved)
                act.wait_ge(dve_moved, t * (SUBS * BATCHES) + moved)
                a, b = h * P // 2, (h + 1) * P // 2
                nc.scalar.copy(pairs_hi[:, :, u * P + a:u * P + b], pairs[u][:, :, a:b]).then_inc(pairs_hi_out, 1)

            def layer_out(t, step):
                bank = step % 2
                act.wait_ge(layer[bank], t * blocks_in(bank, STEPS) + (step // 2 + 1))
                frm = ps_h[bank][:, 0:TILE]
                if step < M1:
                    bias = b1_sb[:, step:step + 1]
                    nc.scalar.activation(r1[:, step, :], frm, ACT.Relu, bias=bias)
                    last = nc.scalar.activation(r1_hi[:, step, :], frm, ACT.Relu, bias=bias)
                elif step < M1 + M2:
                    m = step - M1
                    last = nc.scalar.activation(r2[:, m, :], frm, ACT.Relu, bias=b2_sb[:, m:m + 1])
                else:
                    act.wait_ge(y_sent, t + FREE)
                    last = nc.scalar.copy(y, ps_h[bank][0:1, 0:TILE])
                last.then_inc(layer_read[bank], 1)

            def first_products_out(t, tower=None):
                for k in range(BATCHES):
                    move(t, 0, k)
                    if k == 0 and tower is not None:
                        layer_out(tower, M1 + M2)
                    if k % 2:
                        round_pairs(t, 0, k // 2)
                    for u, g in TURNED_AFTER_BATCH[k]:
                        block_out(t, gathered_block(u, g))

            def second_products_out(t, samples=ACT_SAMPLES):
                for k in range(BATCHES):
                    move(t, 1, k, samples)
                    if k % 2:
                        round_pairs(t, 1, k // 2)

            act.sem_inc(rows_used[0], FREE)
            act.sem_inc(vectors_out[0], FREE)
            act.sem_inc(act_moved, BANKS)
            for bank in range(2):
                act.sem_inc(layer_read[bank], FREE)
            act.dma_start(w3_sb[:], w3).then_inc(small_weights_in, 16)
            act.dma_start(b1_sb[:], b1).then_inc(small_weights_in, 16)
            act.dma_start(b2_sb[:], b2).then_inc(small_weights_in, 16)
            for l in range(NL):
                act.wait_ge(table_in[l], 16)
                nc.scalar.copy(table_hi[:, l], table_raw[l]).then_inc(rounded, 1)
            act.wait_ge(table_split, tables_in_vectors)
            block_out(0, 0)
            act.wait_ge(small_weights_in, 16 * 5)
            nc.scalar.copy(w2_hi[:], w2_raw[:]).then_inc(rounded, 1)
            act.wait_ge(w1_in, 16)
            nc.scalar.copy(w1_hi[:], w1_raw).then_inc(rounded, 1)
            block_out(0, LB - 1)
            for u, g in BEFORE_PRODUCTS:
                block_out(0, gathered_block(u, g))
            dense_out(0)
            act.wait_ge(summed, 1)
            nc.scalar.copy(wd_hi[:], wd_sum[:]).then_inc(rounded, 1)
            act.wait_ge(w1_split, 1)
            first_products_out(0)
            with act.Fori(0, tiles - 1) as t:
                second_products_out(t)
                block_out(t + 1, 0)
                for step in range(M1 + M2):
                    layer_out(t, step)
                    if NL - 1 in LOOKED_UP_AFTER_STEP.get(step, []):
                        block_out(t + 1, LB - 1)
                    if step == M1 - 1:
                        dense_out(t + 1)
                    for u, g in TURNED_AFTER_STEP.get(step, []):
                        block_out(t + 1, gathered_block(u, g))
                first_products_out(t + 1, tower=t)
            second_products_out(tiles - 1, LAST_ACT_SAMPLES)
            for step in range(STEPS):
                layer_out(tiles - 1, step)

        @block.vector
        def _(dve):
            def half_used(t, l, h):
                if ends_block(l) and h == HALVES - 1:
                    b = looked_up_block(l)
                    dve.wait_ge(turned[bank_of(b)], bank_uses(t, b) + 1)
                else:
                    dve.wait_ge(onehot_used, t * (NL * HALVES - LB) + (l * HALVES - l // 2 + h + 1))

            def make_onehot(t, l, halves=range(HALVES), first=False):
                for h in halves:
                    if l >= RING:
                        half_used(t, l - RING, h)
                    elif not first:
                        half_used(t - 1, max(i for i in range(NL) if i % RING == l), h)
                    for c in range(h * HC, (h + 1) * HC):
                        last = nc.vector.tensor_scalar(onehot[:, l % RING, c, :], spread[:, l, :], rown_sb[:, c:c + 1],
                                                       None, ALU.is_equal)
                    last.then_inc(onehot_made, 1)

            def block_out(t, b):
                if bank_of(b) == 1:
                    dve.wait_ge(turned[1], bank_uses(t, b) + 1)
                    if b in LAST_OF_ROWS:
                        dve.sem_inc(rows_used[LAST_OF_ROWS.index(b)], 1)
                    if second_place(b):
                        frm, to = second_place(b)
                        nc.vector.tensor_copy(to, frm)
                    frm, to = block_places(b)
                    nc.vector.tensor_copy(to, frm).then_inc(vectors_out[1], 1)

            def dense_out(t):
                dve.wait_ge(dense_in, t * 16 + 16)
                nc.vector.tensor_copy(vectors[:, :, VECTORS - 1], x[:])
                dve.wait_ge(x_hi_out, t + 1)
                nc.vector.tensor_tensor(x_lo[:], x[:], x_hi[:].bitcast(F32), ALU.subtract).then_inc(x_split, 1)

            def move(t, u, k, samples=DVE_SAMPLES):
                dve.wait_ge(products[k % 2], t * (SUBS * 2) + (u * 2 + k // 2 + 1))
                for g in range(GROUPS):
                    for s in samples:
                        last = nc.vector.tensor_copy(*share(u, k, s, g))
                    if g == 0:
                        last.then_inc(dve_group0, 1)
                dve.wait_ge(dve_group0, t * (SUBS * BATCHES) + (u * BATCHES + k + 1))
                for s in samples:
                    last = nc.vector.tensor_copy(*share_of_first(u, k, s))
                last.then_inc(dve_moved, 1)

            def split_pairs(t, u, h):
                dve.wait_ge(pairs_hi_out, t * (SUBS * 2) + (u * 2 + h + 1))
                a, b = h * P // 2, (h + 1) * P // 2
                nc.vector.tensor_tensor(pairs_lo[:, :, u * P + a:u * P + b], pairs[u][:, :, a:b],
                                        pairs_hi[:, :, u * P + a:u * P + b].bitcast(F32), ALU.subtract
                                        ).then_inc(pairs_split, 1)

            def split_r1(t, m):
                dve.wait_ge(layer_read[m % 2], t * blocks_in(m % 2, STEPS) + (m // 2 + 1 + FREE))
                nc.vector.tensor_tensor(r1_lo[:, m, :], r1[:, m, :], r1_hi[:, m, :].bitcast(F32),
                                        ALU.subtract).then_inc(r1_split, 1)

            def weigh(t, m):
                step = M1 + m
                dve.wait_ge(layer_read[step % 2], t * blocks_in(step % 2, STEPS) + (step // 2 + 1 + FREE))
                w = w3_sb[:, m:m + 1]
                if m == 0:
                    last = nc.vector.tensor_scalar(weighted[:, m, :], r2[:, m, :], w, None, ALU.mult)
                else:
                    dve.wait_ge(r2_weighted, t * M2 + m)
                    last = nc.vector.scalar_tensor_tensor(weighted[:, m, :], r2[:, m, :], w, weighted[:, m - 1, :],
                                                          ALU.mult, ALU.add)
                last.then_inc(r2_weighted, 1)

            def first_products_out(t):
                for k in range(BATCHES):
                    move(t, 0, k)
                    if k == 2:
                        split_pairs(t, 0, 0)
                    for u, g in TURNED_AFTER_BATCH[k]:
                        block_out(t, gathered_block(u, g))

            def second_products_out(t, last=False):
                halves = [] if last else [(l, h) for l in range(2) for h in range(HALVES)]
                for l, h in halves[:1]:
                    make_onehot(t + 1, l, [h])
                split_pairs(t, 0, 1)
                for k in range(BATCHES):
                    move(t, 1, k, LAST_DVE_SAMPLES if last else DVE_SAMPLES)
                    if k == 2:
                        split_pairs(t, 1, 0)
                    for l, h in halves[k + 1:k + 2]:
                        make_onehot(t + 1, l, [h])
                split_pairs(t, 1, 1)

            def split_table(l):
                dve.wait_ge(rounded, l + 1)
                nc.vector.tensor_tensor(table_lo[:, l], table_raw[l], table_hi[:, l].bitcast(F32),
                                        ALU.subtract).then_inc(table_split, 1)

            dve.sem_inc(vectors_out[1], FREE)
            dve.sem_inc(dve_moved, BANKS)
            dve.wait_ge(rown_in, 16)
            dve.wait_ge(spread_in, 16)
            make_onehot(0, 0, first=True)
            split_table(0)
            split_table(1)
            make_onehot(0, 1, first=True)
            split_table(2)
            make_onehot(0, 2)
            split_table(3)
            make_onehot(0, 3)
            split_table(4)
            split_table(5)
            dve.wait_ge(table_split, NL)
            dve.sem_inc(rows_used[1], FREE)
            make_onehot(0, 4)
            make_onehot(0, 5)
            block_out(0, 1)
            nc.vector.memset(vectors[:, :, SECOND + TWICE:SLOT], 0.0).then_inc(pads_zeroed, 1)
            nc.vector.memset(ones[:], 1.0)
            for u, g in BEFORE_PRODUCTS:
                block_out(0, gathered_block(u, g))
            dense_out(0)
            dve.wait_ge(small_weights_in, 16 * 5)
            nc.vector.tensor_tensor(wd_sum[:], wd_raw[:, 0, :], wd_raw[:, 1, :], ALU.add).then_inc(summed, 1)
            dve.wait_ge(rounded, NL + 2)
            nc.vector.tensor_tensor(w1_lo[:], w1_raw, w1_hi[:].bitcast(F32), ALU.subtract).then_inc(w1_split, 1)
            dve.wait_ge(w1_split, 1)
            first_products_out(0)
            nc.vector.tensor_tensor(w2_lo[:], w2_raw[:], w2_hi[:].bitcast(F32), ALU.subtract)
            dve.wait_ge(rounded, NL + 3)
            nc.vector.tensor_tensor(wd_lo[:], wd_sum[:], wd_hi[:].bitcast(F32), ALU.subtract).then_inc(weights_split, 1)
            with dve.Fori(0, tiles - 1) as t:
                dve.wait_ge(spread_in, t * 16 + 32)
                second_products_out(t)
                make_onehot(t + 1, 2)
                make_onehot(t + 1, 3)
                split_r1(t, 0)
                make_onehot(t + 1, 4)
                split_r1(t, 1)
                block_out(t + 1, 1)
                make_onehot(t + 1, 5)
                for step in range(2, M1 + M2):
                    if step < M1:
                        split_r1(t, step)
                    else:
                        weigh(t, step - M1)
                    for u, g in TURNED_AFTER_STEP[step]:
                        block_out(t + 1, gathered_block(u, g))
                    if step == M1 - 1:
                        dense_out(t + 1)
                first_products_out(t + 1)
            second_products_out(tiles - 1, last=True)
            for m in range(M1):
                split_r1(tiles - 1, m)
            for m in range(M2):
                weigh(tiles - 1, m)



def pair_rows():
    row = {}
    at = P + FEATURES
    for i in range(FEATURES):
        row[i, FEATURES] = P + i
        for j in range(i + 1, FEATURES):
            row[i, j] = at
            at += 1

    def row_of(i, j):
        return row[min(ORDER[i], ORDER[j]), max(ORDER[i], ORDER[j])]

    where = np.full((JJ, GROUPS, SLOT), -1)
    for j in range(TWICE, VECTORS):
        for i in range(j):
            where[(j - TWICE) // GROUPS, (j - TWICE) % GROUPS, i if i >= TWICE else SECOND + i] = row_of(i, j)
    for j in range(1, TWICE):
        for i in range(j):
            where[j - 1, 0, i] = row_of(i, j)
    return where.reshape(JJ, P)


def kernel(**inputs):
    import concourse.bacc as bacc
    from concourse.bass_utils import run_bass_kernel_spmd

    a = {k: np.asarray(v) for k, v in inputs.items()}
    where = pair_rows()
    w1 = a["W_top1"]
    w1_pairs = np.zeros((JJ, P, UPPER1), w1.dtype)
    w1_pairs[where >= 0] = w1[where[where >= 0]]
    small = np.zeros((NL, CHUNKS * P, P), np.float32)
    for l, f in enumerate(LOOKED_UP):
        small[l, :len(a[f"tbl_{f}"])] = a[f"tbl_{f}"]
    data = {
        "ids": a["ids"],
        "looked_ids": np.ascontiguousarray(a["ids"][:, LOOKED_UP].T),
        "dense": np.ascontiguousarray(a["r_dense_features"].T),
        "small_tables": np.ascontiguousarray(small.reshape(NL, CHUNKS, P, P).transpose(2, 0, 1, 3)),
        "w1_pairs": np.ascontiguousarray(w1_pairs.transpose(1, 0, 2)),
        "w1_dense": np.stack([w1[:P], w1[-P:]], axis=1),
        "b1": np.ascontiguousarray(a["b_top1"].reshape(M1, P).T),
        "w2": a["W_top2"],
        "b2": np.ascontiguousarray(a["b_top2"].reshape(M2, P).T),
        "w3": np.ascontiguousarray(a["W_top3"].reshape(M2, P).T),
        "eye": np.eye(P, dtype=np.float32),
        "row_numbers": np.arange(CHUNKS * P, dtype=np.float32).reshape(CHUNKS, P).T.copy(),
    }
    for f in GATHERED:
        data[f"tbl_{f}"] = a[f"tbl_{f}"]
    nc = bacc.Bacc("TRN2", target_bir_lowering=False, num_devices=1)
    d = {k: nc.dram_tensor(f"in_{k}", v.shape, mybir.dt.from_np(v.dtype), kind="ExternalInput").ap()
         for k, v in data.items()}
    out = nc.dram_tensor("out_y", (a["ids"].shape[0], 1), F32, kind="ExternalOutput").ap()
    build_dlrm_tower(nc, d["ids"], d["looked_ids"], d["dense"], {f: d[f"tbl_{f}"] for f in GATHERED}, d["small_tables"],
                     d["w1_pairs"], d["w1_dense"], d["b1"], d["w2"], d["b2"], d["w3"], d["eye"],
                     d["row_numbers"], out)
    r = run_bass_kernel_spmd(nc, [{f"in_{k}": v for k, v in data.items()}], core_ids=[0])
    return r.results[0]["out_y"]
```
